# Optimizing a Trainium2 kernel written in Bass

```python
import numpy as np
import jax
import jax.numpy as jnp

def _softmax(x, axis=-1):
    return jax.nn.softmax(x, axis=axis)

def _gelu(x):
    return jax.nn.gelu(x, approximate=True)

def _silu(x):
    return jax.nn.silu(x)

def _sigmoid(x):
    return jax.nn.sigmoid(x)

def _layernorm(x, axis=-1, eps=1e-05):
    m = jnp.mean(x, axis=axis, keepdims=True)
    v = jnp.var(x, axis=axis, keepdims=True)
    return (x - m) / jnp.sqrt(v + eps)

def _scatter_add(tgt, idx, src, axis=0):
    return tgt.at[idx].add(src)

def _segment_sum(src, seg, n):
    return jax.ops.segment_sum(src, seg, n)
kernel_name = 'mk_gnn_resnorm_d2_gnn_r64_106df6'

def setup_inputs(seed: int=0):
    np.random.seed(seed)
    _w = jnp.asarray

    def _rec_inputs():
        import jax
        import jax.numpy as jnp
        _gk = jax.random.key(seed)
        x = -0.0005121 + 1.001 * jax.random.normal(jax.random.fold_in(_gk, 1), (100000, 64), jnp.float32)
        src = jax.random.randint(jax.random.fold_in(_gk, 2), (50000,), 0, 100000, jnp.int32)
        dst = jax.random.randint(jax.random.fold_in(_gk, 3), (50000,), 0, 100000, jnp.int32)
        _o = jnp.argsort(dst, stable=True)
        src = src[_o]
        dst = dst[_o]
        edge_weight = jax.random.uniform(jax.random.fold_in(_gk, 13), (50000,), jnp.float32, 0.0, 0.0625)
        return (x, src, dst, edge_weight)
    x, src, dst, edge_weight = _rec_inputs()

    def _L0_gnn_setup():
        import jax, jax.numpy as jnp
        import numpy as np
        N_NODES = 50000
        N_EDGES = 12500
        D_IN = 64
        D_OUT = 64
        key = jax.random.key(seed)
        k1, k2, k3, k4 = jax.random.split(key, 4)
        x = jax.random.normal(k1, (N_NODES, D_IN), dtype=jnp.float32)
        edge_index = jax.random.randint(k2, (2, N_EDGES), 0, N_NODES, dtype=jnp.int64)
        W_edge = jax.random.normal(k3, (2 * D_IN, D_OUT), dtype=jnp.float32) * (1.0 / np.sqrt(2 * D_IN))
        b_edge = jnp.zeros((D_OUT,), dtype=jnp.float32)
        W_res = jax.random.normal(k4, (D_IN, D_OUT), dtype=jnp.float32) * (1.0 / np.sqrt(D_IN))
        b_res = jnp.zeros((D_OUT,), dtype=jnp.float32)
        return {'x': x, 'edge_index': edge_index, 'W_edge': W_edge, 'b_edge': b_edge, 'W_res': W_res, 'b_res': b_res}
    _L0_gnn_all = _L0_gnn_setup()
    _L0_gnn_in = {k: v for k, v in _L0_gnn_all.items() if k in ('W_edge', 'b_edge', 'W_res', 'b_res')}
    del _L0_gnn_all

    def _L1_gnn_setup():
        import jax, jax.numpy as jnp
        import numpy as np
        N_NODES = 100000
        D_FEAT = 64
        AVG_DEG = 16
        N_EDGES = N_NODES * AVG_DEG

        def _spmm(vals, rows, cols, x, n):
            return jax.ops.segment_sum(vals[:, None] * x[cols], rows, num_segments=n)
        key = jax.random.key(seed)
        k1, k2, k3, k4 = jax.random.split(key, 4)
        rows = jax.random.randint(k1, (N_EDGES,), 0, N_NODES, dtype=jnp.int32)
        cols = jax.random.randint(k2, (N_EDGES,), 0, N_NODES, dtype=jnp.int32)
        vals = jax.random.uniform(k3, (N_EDGES,), dtype=jnp.float32) / AVG_DEG
        x = jax.random.normal(k4, (N_NODES, D_FEAT), dtype=jnp.float32)
        alpha_train = jnp.float32(0.9)
        return {'x': x, 'alpha_train': alpha_train, 'vals': vals, 'rows': rows, 'cols': cols}
    _L1_gnn_all = _L1_gnn_setup()
    _L1_gnn_in = {k: v for k, v in _L1_gnn_all.items() if k in ('alpha_train',)}
    del _L1_gnn_all
    return {'x': x, 'src': src, 'dst': dst, 'edge_weight': edge_weight, 'L0_gnn_W_edge': _L0_gnn_in['W_edge'], 'L0_gnn_b_edge': _L0_gnn_in['b_edge'], 'L0_gnn_W_res': _L0_gnn_in['W_res'], 'L0_gnn_b_res': _L0_gnn_in['b_res'], 'L1_gnn_alpha_train': _L1_gnn_in['alpha_train']}

def reference(x, src, dst, edge_weight, L0_gnn_W_edge, L0_gnn_b_edge, L0_gnn_W_res, L0_gnn_b_res, L1_gnn_alpha_train):
    import jax
    import jax.numpy as jnp

    def _L0_gnn_ref(x, edge_index, W_edge, b_edge, W_res, b_res):
        import jax, jax.numpy as jnp
        import numpy as np
        N_NODES = 50000
        N_EDGES = 12500
        D_IN = 64
        D_OUT = 64
        src, dst = (edge_index[0], edge_index[1])
        x_i = x[dst]
        x_j = x[src]
        msg_in = jnp.concatenate([x_i, x_j - x_i], axis=-1)
        msg = jax.nn.relu(msg_in @ W_edge + b_edge)
        agg = jax.ops.segment_max(msg, dst, num_segments=x.shape[0])
        agg = jnp.where(jnp.isfinite(agg), agg, 0.0)
        return agg + x @ W_res + b_res

    def _L1_gnn_ref(x, alpha_train, vals, rows, cols):
        import jax, jax.numpy as jnp
        import numpy as np
        N_NODES = 100000
        D_FEAT = 64
        AVG_DEG = 16
        N_EDGES = N_NODES * AVG_DEG

        def _spmm(vals, rows, cols, x, n):
            return jax.ops.segment_sum(vals[:, None] * x[cols], rows, num_segments=n)
        n = x.shape[0]
        alph = jnp.clip(jax.nn.sigmoid(alpha_train), 1e-07, 1.0 - 1e-07)
        ax = _spmm(vals, rows, cols, x, n)
        ax = alph * _spmm(vals, rows, cols, ax, n)
        f = ax - x
        f = jnp.nan_to_num(f, nan=0.0, posinf=100000.0, neginf=-100000.0)
        return jnp.clip(f, -10.0, 10.0)
    edge_index = jnp.stack([src, dst])
    x = _layernorm(x + _L0_gnn_ref(x, edge_index, L0_gnn_W_edge, L0_gnn_b_edge, L0_gnn_W_res, L0_gnn_b_res), axis=-1)
    x = _layernorm(x + _L1_gnn_ref(x, L1_gnn_alpha_train, edge_weight, src, dst), axis=-1)
    return x

_drawn_inputs = setup_inputs


def setup_inputs(seed=0):
    import zlib

    import numpy as np

    out = dict(_drawn_inputs(seed))
    spreads = {'L0_gnn_b_edge': (0.0, 0.1), 'L0_gnn_b_res': (0.0, 0.1)}
    factors = {}
    for name, (base, spread) in spreads.items():
        noise = np.random.default_rng([zlib.crc32(name.encode()), seed]).standard_normal(out[name].shape)
        drawn = base * np.exp(spread * noise) if base else spread * noise
        out[name] = jnp.asarray(drawn.astype(out[name].dtype))
    for name, factor in factors.items():
        out[name] = (out[name] * factor).astype(out[name].dtype)
    return out
```

```python
import concourse.bass as bass
from concourse import mybir
from contextlib import ExitStack

P = 128
D = 64
N = 100000
E = 50000
G = 4
EB = G * P
NB = 98
ET = NB * G
C = 784
NPAD = P * C
NU = C // G
NT = P * 800
RING = 4
CH = C // NB
SKIP = 1 << 23
BIG = 3.0e38
FMAX = 3.4028234663852886e38
EPS = 1e-5


def done(b):
    return b + 1


def pair(r, k):
    return 2 * k + r // 2 + 1


def after(eng, sem, value):
    if not (isinstance(value, int) and value <= 0):
        eng.wait_ge(sem, value)


def over(eng, steps, step):
    for r in range(RING):
        step(r, r, 0)
    rounds = steps // RING
    with eng.Fori(1, rounds) as k:
        for r in range(RING):
            step(k * RING + r, r, k)
    for b in range(rounds * RING, steps):
        step(b, b % RING, b // RING)


class Chain:

    def __init__(self, eng, sem):
        self.eng, self.sem, self.base = eng, sem, 0

    def begin(self, b, size):
        self.base, self.size, self.n = b * size, size, 0

    def link(self, ins):
        self.n += 1
        ins.then_inc(self.sem, 1)
        self.eng.wait_ge(self.sem, self.base + self.n)

    def end(self):
        assert self.n == self.size, self.n


def program(nc, x, src_col, dst_col, next_col, w_col, src_row, dst_row, w_edge, b_edge, w_res, b_res, alpha, out):
    fp32, i32, bf16 = mybir.dt.float32, mybir.dt.int32, mybir.dt.bfloat16
    ALU, ACT = mybir.AluOpType, mybir.ActivationFunctionType
    ds = bass.ds

    def at(ap):
        return bass.IndirectOffsetOnAxis(ap=ap, axis=0)

    ctx = ExitStack()
    with ctx:
        def sb(name, shape, dt=fp32):
            return ctx.enter_context(nc.sbuf_tensor(name, shape, dt))

        def ps(name):
            return ctx.enter_context(nc.psum_tensor(name, [P, 512], fp32))

        def sem(name):
            return ctx.enter_context(nc.semaphore(name))

        def sem_ring(name, n=RING):
            return [sem(f"{name}{i}") for i in range(n)]

        def table(name, rows, cols):
            return nc.dram_tensor(name, [rows, cols], fp32, kind="Internal").ap()

        xm, ax, ax2, hd = table("xm", NPAD, 2 * D), table("ax", NT, D), table("ax2", NT, D), table("hd", NPAD, D)
        xm_halves = xm.rearrange("n (k d) -> (n k) d", k=2)

        def by_partition(t, c):
            return t.rearrange("(p c) d -> p c d", p=P) if c is None else t[0:c, :].rearrange("(p c) d -> p c d", p=P)

        x_rows, xm_rows, h_rows, out_rows = (by_partition(t, None) for t in (x, xm, hd, out))
        ax2_rows = by_partition(ax2, NPAD)

        ident = sb("ident", [P, P])
        earlier = sb("earlier", [P, G, EB], bf16)
        w1, w2 = sb("w1", [D, D]), sb("w2", [D, D])
        wcat = sb("wcat", [D + 1, 2 * D])
        zero = sb("zero", [P, 1024])
        alph = sb("alph", [P, 4])
        eps = sb("eps", [P, 1])
        srci, dsti, nexti = sb("srci", [P, ET + G], i32), sb("dsti", [P, ET + G], i32), sb("nexti", [P, ET + G], i32)
        srcf, wcol, seen = sb("srcf", [P, ET + G]), sb("wcol", [P, ET + G]), sb("seen", [P, ET + G])
        addi, maxi = sb("addi", [P, ET + G], i32), sb("maxi", [P, ET + G], i32)

        idx, sidx = sb("idx", [P, RING, G], i32), sb("sidx", [P, RING, G], i32)
        rows = sb("rows", [P, RING, G, 2 * D])
        srow = sb("srow", [P, RING, EB], i32)
        xT = sb("xT", [D + 1, 2, EB])
        sums = sb("sums", [P, 2, G, D])
        same = sb("same", [P, 2, G, EB])
        dwin = sb("dwin", [D, RING, EB + 1], i32)
        pen = sb("pen", [D, 2, EB])
        run = sb("run", [D, 2, EB])
        junk = sb("junk", [P, EB])
        xbuf = same[:, :, :, :].rearrange("p a g e -> p (a g e)").rearrange("p (r c d) -> p r c d", r=RING, c=CH)
        store = sb("store", [P, ET * D])
        used = [0]

        def carve(parts, *shape):
            size = 1
            for s in shape:
                size *= s
            lo = used[0]
            used[0] += size
            assert used[0] <= ET * D
            names = "abcd"[:len(shape)]
            spec = f"p ({' '.join(names)}) -> p {' '.join(names)}"
            return store[0:parts, lo:lo + size].rearrange(spec, **dict(zip(names, shape)))

        dx, dh = carve(P, RING, G, 2 * D), carve(P, RING, G, D)
        dxT = carve(D + 1, 2, EB)
        vals = carve(P, 2, G, D)
        tmp = [carve(P, 4, G * D) for _ in range(2)]
        stats = [carve(P, G, 6) for _ in range(2)]
        mv = [carve(P, G, 2) for _ in range(2)]
        rstd = [carve(P, 3, G) for _ in range(2)]

        pT, pDT, pM, pDM = ps("pT"), ps("pDT"), ps("pM"), ps("pDM")
        pS = [ps("pS0"), ps("pS1")]
        pB = [pM, pDM]

        loaded, prep, consts_made, sums_made, zero_made = (sem(n) for n in ("loaded", "prep", "consts_made", "sums_made", "zero_made"))
        tables_zeroed, wcat_made, alpha_exp, alpha_made = (sem(n) for n in ("tables_zeroed", "wcat_made", "alpha_exp", "alpha_made"))
        set_up, holds = sem("set_up"), sem("holds")
        p1_gath, p1_dwin, p1_srow = sem_ring("p1_gath"), sem_ring("p1_dwin"), sem_ring("p1_srow")
        xm_in, xm_out = sem_ring("xm_in"), sem_ring("xm_out")
        p1_xT, p1_xTs, p1_b, p1_run, p1_back, p1_store, p1_idx, p1_seen, p1_chain = (
            sem(n) for n in ("p1_xT", "p1_xTs", "p1_b", "p1_run", "p1_back", "p1_store", "p1_idx", "p1_seen", "p1_chain"))
        index_chain, m_ring, m_idx, m_tick = (sem(n) for n in ("index_chain", "m_ring", "m_idx", "m_tick"))
        m_sc = sem_ring("m_sc", 2)
        phase = {}
        for ph in "ab":
            s = {n: sem_ring(f"{ph}_{n}") for n in ("gath", "srow", "din", "dout")}
            s.update({n: sem(f"{ph}_{n}") for n in (
                "xT", "xTs", "mm", "mused", "dxT", "dxTs", "dmm", "dmused", "dread", "var", "dvar", "sd", "dsd",
                "same", "vals", "sum", "sums", "idx", "sidx", "sc", "landed", "dh", "chain")})
            phase[ph] = s
        f_in, f_out = sem_ring("f_in"), sem_ring("f_out")
        f_var, f_sd, f_done, f_chain, sums_in = (sem(n) for n in ("f_var", "f_sd", "f_done", "f_chain", "sums_in"))
        block = ctx.enter_context(nc.Block())

        @block.sync
        def _(sp):
            for dram, tile in ((src_col, srci[:, :]), (dst_col, dsti[:, :]), (next_col, nexti[:, :]), (w_col, wcol[:, :]),
                               (w_edge[0:D, :], w1[:, :]), (w_edge[D:2 * D, :], w2[:, :]), (w_res, wcat[0:D, D:2 * D]),
                               (b_edge, wcat[D:D + 1, 0:D]), (b_res, wcat[D:D + 1, D:2 * D]),
                               (alpha.to_broadcast([P, 1]), alph[:, 0:1])):
                sp.dma_start(tile, dram).then_inc(loaded, 16)

            def windows(b, r, k):
                after(sp, p1_run, done(b - RING))
                sp.dma_start(dwin[:, r, :], dst_row[:, ds(b * EB, EB + 1)].to_broadcast([D, EB + 1])).then_inc(p1_dwin[r], 16)
                after(sp, p1_seen, done(b - RING))
                sp.dma_start(srow[:, r, :], src_row[:, ds(b * EB, EB)].to_broadcast([P, EB])).then_inc(p1_srow[r], 16)
                after(sp, xm_out[r], 16 * k)
                sp.dma_start(xbuf[:, r, :, 0:D], x_rows[:, ds(b * CH, CH), :]).then_inc(xm_in[r], 16)
            over(sp, NB, windows)

            for n, ph in enumerate("ab"):
                s = phase[ph]
                if ph == "a":
                    for q in range(2):
                        sp.wait_ge(m_sc[q], 64 * NB // 2)
                    sp.wait_ge(p1_seen, NB)

                def store_h(b, r, k):
                    sp.wait_ge(s["dh"], done(b))
                    sp.dma_start(h_rows[:, ds((b + n * NB) * G, G), :], dh[:, r, :, :]).then_inc(s["dout"][r], 16)

                def feed(b, r, k):
                    after(sp, s["same"], done(b - RING))
                    sp.dma_start(srow[:, r, :], src_row[:, ds(b * EB, EB)].to_broadcast([P, EB])).then_inc(s["srow"][r], 16)
                    after(sp, s["dread"], done(b - RING))
                    sp.dma_start(dx[:, r, :, :], xm_rows[:, ds((b + n * NB) * G, G), :]).then_inc(s["din"][r], 16)
                    if not (isinstance(b, int) and b < RING):
                        store_h(b - RING, r, k)
                over(sp, NB, feed)
                for b in range(NB - RING, NB):
                    store_h(b, b % RING, b // RING)
                for r in range(RING):
                    sp.wait_ge(s["dout"][r], 16 * ((NB - r + RING - 1) // RING))

            sp.wait_ge(sums_in, 1)

            def load(b, r, k):
                after(sp, f_done, done(b - RING))
                sp.dma_start(dx[:, r, :, 0:D], h_rows[:, ds(b * G, G), :]).then_inc(f_in[r], 16)
                sp.dma_start(dx[:, r, :, D:2 * D], ax2_rows[:, ds(b * G, G), :]).then_inc(f_in[r], 16)
            over(sp, NU, load)

        @block.gpsimd
        def _(pool):
            def hold(sem, value):
                pool.wait_ge(sem, value)
                pool.sem_inc(holds, 1)

            nc.gpsimd.memset(ident[:, :], 0.0).then_inc(prep, 1)
            nc.gpsimd.memset(earlier[:, :, :], 1.0).then_inc(prep, 1)
            pool.wait_ge(prep, 2)
            nc.gpsimd.affine_select(out=ident[:, :], in_=ident[:, :], compare_op=ALU.not_equal, fill=1.0, base=0,
                                    pattern=[[-1, P]], channel_multiplier=1).then_inc(consts_made, 1)
            nc.gpsimd.affine_select(out=earlier[:, :, :], in_=earlier[:, :, :], compare_op=ALU.is_gt, fill=0.0, base=0,
                                    pattern=[[P, G], [-1, EB]], channel_multiplier=1).then_inc(consts_made, 1)
            nc.gpsimd.iota(addi[:, :].rearrange("p (b g) -> p b g", g=G), pattern=[[0, NB + 1], [P, G]], base=NPAD,
                           channel_multiplier=1).then_inc(consts_made, 1)

            def gather_x(b, r, k):
                hold(p1_idx, done(b))
                for g in range(G):
                    nc.gpsimd.indirect_dma_start(rows[:, r, g, 0:D], None, x, at(idx[:, r, g:g + 1])).then_inc(p1_gath[r], 16)
            over(pool, NB, gather_x)

            for r in range(RING):
                pool.wait_ge(xm_out[r], 16 * ((NB - r + RING - 1) // RING))

            def put_max(b, r, k):
                hold(m_ring, done(b))
                hold(m_idx, done(b))
                for g in range(G):
                    nc.gpsimd.indirect_dma_start(xm_halves, at(sidx[:, r, g:g + 1]), sums[:, r % 2, g, :], None,
                                                 bounds_check=2 * NPAD - 1, oob_is_err=False).then_inc(m_sc[r % 2], 16)
                if not (isinstance(b, int) and b == 0):
                    hold(m_sc[1 - r % 2], 64 * pair(r - 1, k))
                    pool.sem_inc(m_tick, 1)
            over(pool, NB, put_max)
            for q in range(2):
                pool.wait_ge(m_sc[q], 64 * NB // 2)
            pool.sem_inc(m_tick, 1)
            pool.wait_ge(tables_zeroed, 32)

            for ph, source, width, target in (("a", xm, 2 * D, ax), ("b", ax, D, ax2)):
                s = phase[ph]

                def gather(r, b):
                    hold(s["idx"], done(b))
                    for g in range(G):
                        nc.gpsimd.indirect_dma_start(rows[:, r, g, 0:width], None, source,
                                                     at(idx[:, r, g:g + 1])).then_inc(s["gath"][r], 16)

                gather(0, 0)
                gather(1, 1)

                def turn(b, r, k):
                    if not (isinstance(b, int) and b + 2 >= NB):
                        gather((r + 2) % RING, b + 2)
                    if not (isinstance(b, int) and b == 0):
                        pool.wait_ge(s["sc"], 64 * b)
                        pool.sem_inc(s["landed"], 1)
                    hold(s["sums"], done(b))
                    hold(s["sidx"], done(b))
                    for g in range(G):
                        nc.gpsimd.indirect_dma_start(target, at(sidx[:, r, g:g + 1]), sums[:, r % 2, g, :], None,
                                                     compute_op=ALU.add).then_inc(s["sc"], 16)
                over(pool, NB, turn)
                pool.wait_ge(s["sc"], 64 * NB)
                pool.sem_inc(s["landed"], 1)
            pool.sem_inc(sums_in, 1)

        @block.scalar
        def _(act):
            act.wait_ge(loaded, 160)
            nc.scalar.activation(alph[:, 1:2], alph[:, 0:1], ACT.Exp, scale=-1.0).then_inc(alpha_exp, 1)
            act.wait_ge(zero_made, 1)
            for t in (ax, ax2):
                act.dma_start(t.rearrange("(p k c) d -> p k (c d)", p=P, c=16),
                              zero[:, :].rearrange("p (o c) -> p o c", o=1).to_broadcast([P, NT // P // 16, 1024])).then_inc(tables_zeroed, 16)
            act.wait_ge(set_up, 1)

            def back(b, r, k):
                act.wait_ge(p1_back, done(b))
                nc.scalar.activation(store[:, ds(b * (G * D), G * D)], pS[r % 2][:, 0:G * D], ACT.Copy).then_inc(p1_store, 1)

            def evac(b, r, k):
                q = r % 2
                act.wait_ge(xm_in[r], 16 * (k + 1))
                act.dma_start(xm_rows[:, ds(b * CH, CH), :], xbuf[:, r, :, :]).then_inc(xm_out[r], 16)
                act.wait_ge(p1_xT, done(b))
                after(act, p1_b, done(b - 2))
                nc.scalar.activation(xT[0:D, q, :], pT[0:D, :], ACT.Copy).then_inc(p1_xTs, 1)
                if not (isinstance(b, int) and b == 0):
                    back(b - 1, (r - 1) % RING, k)
            over(act, NB, evac)
            back(NB - 1, (NB - 1) % RING, 0)
            act.wait_ge(p1_store, NB)

            def stage(b, r, k):
                after(act, m_tick, done(b - 2))
                nc.scalar.activation(sums[:, r % 2, :, :].rearrange("p g d -> p (g d)"), store[:, ds(b * (G * D), G * D)],
                                     ACT.Copy).then_inc(m_ring, 1)
            over(act, NB, stage)

            for ph in "ab":
                s = phase[ph]

                def sums_out(b, r, k):
                    act.wait_ge(s["sum"], done(b))
                    after(act, s["landed"], done(b - 2))
                    nc.scalar.activation(sums[:, r % 2, :, :].rearrange("p g d -> p (g d)"), pS[r % 2][:, 0:G * D],
                                         ACT.Copy).then_inc(s["sums"], 1)

                def step(b, r, k):
                    q = r % 2
                    if ph == "a":
                        act.wait_ge(s["xT"], done(b))
                        after(act, s["mm"], done(b - 2))
                        nc.scalar.activation(xT[0:D, q, :], pT[0:D, :], ACT.Copy).then_inc(s["xTs"], 1)
                    act.wait_ge(s["dxT"], done(b))
                    after(act, s["dmm"], done(b - 2))
                    nc.scalar.activation(dxT[0:D, q, :], pDT[0:D, :], ACT.Copy).then_inc(s["dxTs"], 1)
                    if not (isinstance(b, int) and b == 0):
                        sums_out(b - 1, (r - 1) % RING, k)
                    if ph == "a":
                        act.wait_ge(s["var"], done(b))
                        nc.scalar.activation(rstd[0][:, 0, :], mv[0][:, :, 1], ACT.Sqrt, bias=eps[:, 0:1]).then_inc(s["sd"], 1)
                    act.wait_ge(s["dvar"], done(b))
                    nc.scalar.activation(rstd[1][:, 0, :], mv[1][:, :, 1], ACT.Sqrt, bias=eps[:, 0:1]).then_inc(s["dsd"], 1)
                if ph == "a":
                    act.wait_ge(m_tick, NB)
                over(act, NB, step)
                sums_out(NB - 1, (NB - 1) % RING, 0)

            def last(b, r, k):
                act.wait_ge(f_var, done(b))
                nc.scalar.activation(rstd[1][:, 0, :], mv[1][:, :, 1], ACT.Sqrt, bias=eps[:, 0:1]).then_inc(f_sd, 1)
                act.wait_ge(f_done, done(b))
                act.dma_start(out_rows[:, ds(b * G, G), :], dh[:, r, :, :]).then_inc(f_out[r], 16)
            over(act, NU, last)
            for r in range(RING):
                act.wait_ge(f_out[r], 16 * (NU // RING))

        @block.vector
        def _(dve):
            v = nc.vector
            nc.vector.memset(zero[:, :], 0.0).then_inc(zero_made, 1)
            v.memset(eps[:, :], EPS)
            v.memset(xT[D:D + 1, :, :], 1.0)
            v.memset(xbuf[:, :, :, D:2 * D], -BIG).then_inc(set_up, 1)
            dve.wait_ge(loaded, 160)
            v.tensor_tensor(wcat[0:D, 0:D], w1[:, :], w2[:, :], ALU.subtract).then_inc(wcat_made, 1)
            dve.wait_ge(alpha_exp, 1)
            ch = Chain(dve, alpha_made)
            ch.begin(0, 3)
            ch.link(v.tensor_scalar_add(alph[:, 2:3], alph[:, 1:2], 1.0))
            ch.link(v.reciprocal(alph[:, 3:4], alph[:, 2:3]))
            ch.link(v.tensor_scalar(alph[:, 2:3], alph[:, 3:4], 1e-7, 1.0 - 1e-7, ALU.max, ALU.min))
            ch.end()
            dve.wait_ge(consts_made, 3)
            ch = Chain(dve, index_chain)
            ch.begin(0, 5)
            ch.link(v.tensor_copy(srcf[:, :], srci[:, :]))
            ch.link(v.tensor_tensor(seen[:, :], nexti[:, :], dsti[:, :], ALU.not_equal))
            ch.link(v.tensor_scalar(maxi[:, :], dsti[:, :], 2.0, float(1 - SKIP), ALU.mult, ALU.add))
            ch.link(v.tensor_tensor(maxi[:, :], maxi[:, :], seen[:, :], ALU.mult))
            ch.link(v.tensor_scalar(maxi[:, :], maxi[:, :], 1.0, float(SKIP), ALU.mult, ALU.add))
            ch.end()

            def columns(ring, source, b, r, sem):
                if isinstance(b, int) and b >= NB:
                    return
                v.tensor_copy(ring[:, r, :], source[:, ds(b * G, G)]).then_inc(sem, 1)

            for b in range(3):
                columns(idx, srci, b, b, p1_idx)
            ch = Chain(dve, p1_chain)

            def scan(b, r, k):
                q = r % 2
                ch.begin(b, 6)
                columns(idx, srci, b + 3, (r + 3) % RING, p1_idx)
                dve.wait_ge(p1_srow[r], 16 * (k + 1))
                for g in range(G):
                    w = (g + 1) * P
                    ins = v.scalar_tensor_tensor(out=junk[:, 0:w], in0=srow[:, r, 0:w], scalar=srcf[:, ds(b * G + g, 1)],
                                                 in1=earlier[:, g, 0:w], op0=ALU.is_equal, op1=ALU.mult,
                                                 accum_out=seen[:, ds(b * G + g, 1)])
                    ch.link(ins)
                v.sem_inc(p1_seen, 1)
                dve.wait_ge(p1_dwin[r], 16 * (k + 1))
                ch.link(v.tensor_tensor(pen[:, q, :], dwin[:, r, 0:EB], dwin[:, r, 1:EB + 1], ALU.subtract))
                ch.link(v.tensor_scalar(pen[:, q, :], pen[:, q, :], -1.0, BIG, ALU.max, ALU.mult))
                dve.wait_ge(p1_b, done(b))
                after(dve, p1_back, done(b - 2))
                first = isinstance(b, int) and b == 0
                v.tensor_tensor_scan(run[:, q, :], pen[:, q, :], pB[q][0:D, :],
                                     -BIG if first else run[:, 1 - q, EB - 1:EB], ALU.add, ALU.max).then_inc(p1_run, 1)
                dve.wait_ge(p1_run, done(b))
                ch.end()
            over(dve, NB, scan)

            ch = Chain(dve, index_chain)
            ch.base, ch.size, ch.n = 5, 4, 0
            v.memset(seen[:, ET:ET + G], 0.0)
            ch.link(v.tensor_scalar(seen[:, 0:ET], seen[:, 0:ET], 1.0, None, ALU.min))
            ch.link(v.tensor_tensor(srcf[:, :], addi[:, :], srcf[:, :], ALU.subtract))
            ch.link(v.tensor_tensor(srcf[:, :], srcf[:, :], seen[:, :], ALU.mult))
            ch.link(v.tensor_tensor(addi[:, :], srcf[:, :], srci[:, :], ALU.add))
            ch.end()
            v.tensor_copy(srcf[:, :], srci[:, :]).then_inc(sums_made, 1)
            dve.wait_ge(sums_made, 1)

            def max_columns(b, r, k):
                after(dve, m_tick, done(b - RING))
                columns(sidx, maxi, b, r, m_idx)
            over(dve, NB, max_columns)
            for q in range(2):
                dve.wait_ge(m_sc[q], 64 * NB // 2)
            v.memset(dxT[D:D + 1, :, :], 1.0).then_inc(set_up, 1)

            for n, ph in enumerate("ab"):
                s = phase[ph]
                ch = Chain(dve, s["chain"])
                if ph == "b":
                    dve.wait_ge(phase["a"]["landed"], NB)
                for b in range(3):
                    columns(idx, dsti, b, b, s["idx"])

                def node_sum(rows_in, product, i, used_up):
                    p4 = product[:, :].rearrange("p (g d) -> p g d", g=G)
                    t = tmp[i]
                    t4 = [t[:, j, :].rearrange("p (g d) -> p g d", g=G) for j in range(4)]
                    v.tensor_tensor(t4[1], p4[:, :, D:2 * D], rows_in[:, :, 0:D], ALU.add)
                    ins = v.tensor_tensor(t4[0], p4[:, :, 0:D], rows_in[:, :, D:2 * D], ALU.add)
                    ch.link(ins)
                    v.sem_inc(used_up, 1)
                    ch.link(v.tensor_scalar(t[:, 2, :], t[:, 0, :], FMAX, None, ALU.is_le))
                    ch.link(v.scalar_tensor_tensor(out=t[:, 3, :], in0=t[:, 0, :], scalar=FMAX, in1=t[:, 2, :], op0=ALU.min, op1=ALU.mult))
                    ch.link(v.scalar_tensor_tensor(out=t[:, 0, :], in0=t[:, 3, :], scalar=0.0, in1=t[:, 1, :], op0=ALU.max, op1=ALU.add))
                    moments(ch, t[:, 0, :], i)

                def moments(ch, u, i):
                    for g in range(G):
                        ins = v.bn_stats(stats[i][:, g, :], u[:, g * D:(g + 1) * D])
                    ch.link(ins)
                    v.sem_inc(holds, 1)
                    for g in range(G):
                        ins = v.bn_aggr(mv[i][:, g, :], stats[i][:, g, :])
                    ch.link(ins)

                def scaled(u, i, factor, dest, sem):
                    for g in range(G):
                        ins = v.tensor_scalar(dest[:, g, :], u[:, g * D:(g + 1) * D], mv[i][:, g, 0:1], factor[:, g:g + 1],
                                              ALU.subtract, ALU.mult)
                    ins.then_inc(sem, 1)

                def step(b, r, k):
                    q = r % 2
                    ch.begin(b, 15 if ph == "a" else 8)
                    columns(idx, dsti, b + 3, (r + 3) % RING, s["idx"])
                    after(dve, s["landed"], done(b - RING))
                    columns(sidx, addi, b, r, s["sidx"])
                    dve.wait_ge(s["srow"][r], 16 * (k + 1))
                    after(dve, s["sum"], done(b - 2))
                    for g in range(G):
                        ins = v.tensor_scalar(same[:, q, g, :], srow[:, r, :], srcf[:, ds(b * G + g, 1)], None, ALU.is_equal)
                    ins.then_inc(s["same"], 1)
                    if ph == "a":
                        dve.wait_ge(s["mm"], done(b))
                        node_sum(rows[:, r, :, :], pM, 0, s["mused"])
                        v.sem_inc(s["var"], 1)
                    else:
                        dve.wait_ge(s["gath"][r], 64 * (k + 1))
                        v.tensor_tensor(vals[:, q, :, :], rows[:, r, :, 0:D],
                                        wcol[:, ds(b * G, G)].rearrange("p (g o) -> p g o", o=1).to_broadcast([P, G, D]),
                                        ALU.mult).then_inc(s["vals"], 1)
                    dve.wait_ge(s["dmm"], done(b))
                    node_sum(dx[:, r, :, :], pDM, 1, s["dmused"])
                    v.sem_inc(s["dvar"], 1)
                    v.sem_inc(s["dread"], 1)
                    if ph == "a":
                        dve.wait_ge(s["sd"], done(b))
                        ch.link(v.reciprocal(rstd[0][:, 1, :], rstd[0][:, 0, :]))
                        ch.link(v.tensor_tensor(rstd[0][:, 2, :], rstd[0][:, 1, :], wcol[:, ds(b * G, G)], ALU.mult))
                        scaled(tmp[0][:, 0, :], 0, rstd[0][:, 2, :], vals[:, q, :, :], s["vals"])
                    dve.wait_ge(s["dsd"], done(b))
                    ch.link(v.reciprocal(rstd[1][:, 1, :], rstd[1][:, 0, :]))
                    after(dve, s["dout"][r], 16 * k)
                    scaled(tmp[1][:, 0, :], 1, rstd[1][:, 1, :], dh[:, r, :, :], s["dh"])
                    dve.wait_ge(s["dh"], done(b))
                    if ph == "b":
                        ch.link(v.tensor_copy(rstd[1][:, 2, :], rstd[1][:, 1, :]))
                    ch.end()
                over(dve, NB, step)

            ch = Chain(dve, f_chain)

            def last(b, r, k):
                ch.begin(b, 8)
                t = tmp[1]
                t4 = [t[:, j, :].rearrange("p (g d) -> p g d", g=G) for j in range(4)]
                dve.wait_ge(f_in[r], 32 * (k + 1))
                ch.link(v.scalar_tensor_tensor(out=t4[0], in0=dx[:, r, :, D:2 * D], scalar=alph[:, 2:3], in1=dx[:, r, :, 0:D],
                                               op0=ALU.mult, op1=ALU.subtract))
                v.tensor_tensor(t[:, 1, :], t[:, 0, :], t[:, 0, :], ALU.is_equal)
                ch.link(v.tensor_scalar(t[:, 2, :], t[:, 0, :], -10.0, 10.0, ALU.max, ALU.min))
                ch.link(v.tensor_tensor(t[:, 3, :], t[:, 2, :], t[:, 1, :], ALU.mult))
                ch.link(v.tensor_tensor(t4[0], t4[3], dx[:, r, :, 0:D], ALU.add))
                for g in range(G):
                    ins = v.bn_stats(stats[1][:, g, :], t[:, 0, g * D:(g + 1) * D])
                ch.link(ins)
                v.sem_inc(holds, 1)
                for g in range(G):
                    ins = v.bn_aggr(mv[1][:, g, :], stats[1][:, g, :])
                ch.link(ins)
                v.sem_inc(f_var, 1)
                dve.wait_ge(f_sd, done(b))
                ch.link(v.reciprocal(rstd[1][:, 1, :], rstd[1][:, 0, :]))
                after(dve, f_out[r], 16 * k)
                for g in range(G):
                    ins = v.tensor_scalar(dh[:, r, g, :], t[:, 0, g * D:(g + 1) * D], mv[1][:, g, 0:1], rstd[1][:, 1, g:g + 1],
                                          ALU.subtract, ALU.mult)
                ch.link(ins)
                v.sem_inc(f_done, 1)
                ch.end()
            over(dve, NU, last)

        @block.tensor
        def _(pe):
            pe.wait_ge(consts_made, 3)
            pe.wait_ge(loaded, 160)
            pe.wait_ge(set_up, 1)
            pe.wait_ge(wcat_made, 1)

            def hold(sem, value):
                if not (isinstance(value, int) and value <= 0):
                    pe.wait_ge(sem, value)
                    pe.sem_inc(holds, 1)

            def turn_back(b, r, k):
                q = r % 2
                hold(p1_run, done(b))
                hold(p1_store, done(b - 2))
                for g in range(G):
                    ins = nc.tensor.transpose(pS[q][:, g * D:(g + 1) * D], run[:, q, g * P:(g + 1) * P], ident[0:D, 0:D])
                ins.then_inc(p1_back, 1)

            def first(b, r, k):
                q = r % 2
                hold(p1_gath[r], 64 * (k + 1))
                hold(p1_xTs, done(b - 1))
                for g in range(G):
                    ins = nc.tensor.transpose(pT[0:D, g * P:(g + 1) * P], rows[:, r, g, 0:D], ident[:, :])
                ins.then_inc(p1_xT, 1)
                hold(p1_xTs, done(b))
                hold(p1_run, done(b - 2))
                nc.tensor.matmul(pB[q][0:D, :], w2[:, :], xT[0:D, q, :], start=True, stop=True).then_inc(p1_b, 1)
                if not (isinstance(b, int) and b == 0):
                    turn_back(b - 1, (r - 1) % RING, k)
            over(pe, NB, first)
            turn_back(NB - 1, (NB - 1) % RING, 0)
            pe.wait_ge(set_up, 2)

            for ph in "ab":
                s = phase[ph]

                def add_up(b, r, k):
                    q = r % 2
                    hold(s["vals"], done(b))
                    hold(s["sums"], done(b - 2))
                    for i in range(G):
                        for j in range(G):
                            ins = nc.tensor.matmul(pS[q][:, i * D:(i + 1) * D], same[:, q, j, i * P:(i + 1) * P],
                                                   vals[:, q, j, :], start=(j == 0), stop=(j == G - 1))
                    ins.then_inc(s["sum"], 1)

                def products(b, r, rows_in, arrived, amount, pt, t_made, t_out, ts, pm, used_up, made):
                    hold(arrived, amount)
                    hold(t_out, done(b - 1))
                    for g in range(G):
                        ins = nc.tensor.transpose(pt[0:D, g * P:(g + 1) * P], rows_in[:, g, 0:D], ident[:, :])
                    ins.then_inc(t_made, 1)
                    hold(t_out, done(b))
                    hold(used_up, done(b - 1))
                    for g in range(G):
                        ins = nc.tensor.matmul(pm[:, g * 2 * D:(g + 1) * 2 * D], ts[:, g * P:(g + 1) * P], wcat[:, :],
                                               start=True, stop=True)
                    ins.then_inc(made, 1)

                def step(b, r, k):
                    q = r % 2
                    if ph == "a":
                        products(b, r, rows[:, r, :, :], s["gath"][r], 64 * (k + 1), pT, s["xT"], s["xTs"], xT[:, q, :], pM,
                                 s["mused"], s["mm"])
                    products(b, r, dx[:, r, :, :], s["din"][r], 16 * (k + 1), pDT, s["dxT"], s["dxTs"], dxT[:, q, :], pDM,
                             s["dmused"], s["dmm"])
                    if not (isinstance(b, int) and b == 0):
                        add_up(b - 1, (r - 1) % RING, k)
                over(pe, NB, step)
                add_up(NB - 1, (NB - 1) % RING, 0)


def kernel(x, src, dst, edge_weight, L0_gnn_W_edge, L0_gnn_b_edge, L0_gnn_W_res, L0_gnn_b_res, L1_gnn_alpha_train):
    import numpy as np
    import concourse.bacc as bacc
    from concourse.bass_utils import run_bass_kernel_spmd

    def padded(a, length, fill):
        full = np.full((length,), fill, a.dtype)
        full[:a.shape[0]] = a
        return full

    def columns(a):
        return np.ascontiguousarray(a.reshape(ET + G, P).T)

    x, src, dst, w = (np.asarray(a) for a in (x, src, dst, edge_weight))
    long = (ET + G) * P
    x_full = np.zeros((NPAD, D), x.dtype)
    x_full[:N] = x
    src_p, dst_p, w_p = padded(src, long, 0), padded(dst, long + 1, N), padded(w, long, 0)
    next_p = dst_p[1:].copy()
    next_p[ET * P - 1:] = N + 1
    before = np.full((1, ET * P + 1), -1, dst.dtype)
    before[0, 1:] = dst_p[:ET * P]
    arrays = {
        "x": x_full, "src_col": columns(src_p), "dst_col": columns(dst_p[:long]), "next_col": columns(next_p), "w_col": columns(w_p),
        "src_row": src_p[:ET * P].reshape(1, -1), "dst_row": before,
        "w_edge": np.asarray(L0_gnn_W_edge), "b_edge": np.asarray(L0_gnn_b_edge).reshape(1, D),
        "w_res": np.asarray(L0_gnn_W_res), "b_res": np.asarray(L0_gnn_b_res).reshape(1, D),
        "alpha": np.asarray(L1_gnn_alpha_train).reshape(1, 1),
    }
    arrays = {f"in_{n}": np.ascontiguousarray(a) for n, a in arrays.items()}
    nc = bacc.Bacc("TRN2", target_bir_lowering=False, num_devices=1)
    args = [nc.dram_tensor(n, a.shape, mybir.dt.from_np(a.dtype), kind="ExternalInput").ap() for n, a in arrays.items()]
    out = nc.dram_tensor("out", (NPAD, D), mybir.dt.float32, kind="ExternalOutput").ap()
    program(nc, *args, out)
    got = run_bass_kernel_spmd(nc, [arrays], core_ids=[0]).results[0]["out"]
    return got[:N]
```

```python
import concourse.bass as bass
from concourse import mybir
from contextlib import ExitStack

P = 128
D = 64
N = 100000
E = 50000
G = 4
EB = G * P
NB = 98
ET = NB * G
C = 784
NPAD = P * C
H2 = 2 * G
NT = NPAD + EB
RING = 4
CH = C // NB
LAST = ET + 2 * G
SKIP = 1 << 23
BIG = 3.0e38
FMAX = 3.4028234663852886e38
EPS = 1e-5


def done(b):
    return b + 1


def pair(r, k):
    return 2 * k + r // 2 + 1


def after(eng, sem, value):
    if not (isinstance(value, int) and value <= 0):
        eng.wait_ge(sem, value)


def over(eng, steps, step, peel=1):
    rounds = steps // RING
    for b in range(peel * RING):
        step(b, b % RING, b // RING)
    with eng.Fori(peel, rounds) as k:
        for r in range(RING):
            step(k * RING + r, r, k)
    for b in range(rounds * RING, steps):
        step(b, b % RING, b // RING)


class Chain:

    def __init__(self, eng, sem):
        self.eng, self.sem, self.base = eng, sem, 0

    def begin(self, b, size):
        self.base, self.size, self.n = b * size, size, 0

    def link(self, ins):
        self.n += 1
        ins.then_inc(self.sem, 1)
        self.eng.wait_ge(self.sem, self.base + self.n)

    def end(self):
        assert self.n == self.size, self.n


def program(nc, x, src_col, dst_col, next_col, w_col, src_row, dst_row, w_edge, b_edge, w_res, b_res, alpha, out):
    fp32, i32, bf16 = mybir.dt.float32, mybir.dt.int32, mybir.dt.bfloat16
    ALU, ACT = mybir.AluOpType, mybir.ActivationFunctionType
    ds = bass.ds

    def at(ap):
        return bass.IndirectOffsetOnAxis(ap=ap, axis=0)

    ctx = ExitStack()
    with ctx:
        def sb(name, shape, dt=fp32):
            return ctx.enter_context(nc.sbuf_tensor(name, shape, dt))

        def ps(name):
            return ctx.enter_context(nc.psum_tensor(name, [P, 512], fp32))

        def sem(name):
            return ctx.enter_context(nc.semaphore(name))

        def sem_ring(name, n=RING):
            return [sem(f"{name}{i}") for i in range(n)]

        def table(name, rows, cols):
            return nc.dram_tensor(name, [rows, cols], fp32, kind="Internal").ap()

        xm, ax, ax2, hd = table("xm", NPAD, 2 * D), table("ax", NT, D), table("ax2", NT, D), table("hd", NPAD, D)
        xm_halves = xm.rearrange("n (k d) -> (n k) d", k=2)

        def by_partition(t, c):
            return t.rearrange("(p c) d -> p c d", p=P) if c is None else t[0:c, :].rearrange("(p c) d -> p c d", p=P)

        x_rows, xm_rows, h_rows, out_rows = (by_partition(t, None) for t in (x, xm, hd, out))
        ax2_rows = by_partition(ax2, NPAD)

        ident = sb("ident", [P, P])
        earlier = sb("earlier", [P, G, EB], bf16)
        w1, w2 = sb("w1", [D, D]), sb("w2", [D, D])
        wcat = sb("wcat", [D + 1, 2 * D])
        zero = sb("zero", [P, CH * D])
        alph = sb("alph", [P, 4])
        eps = sb("eps", [P, 1])
        srci, dsti, nexti = sb("srci", [P, LAST], i32), sb("dsti", [P, LAST], i32), sb("nexti", [P, LAST], i32)
        srcf, wcol, seen = sb("srcf", [P, LAST]), sb("wcol", [P, LAST]), sb("seen", [P, LAST])
        addi, maxi = sb("addi", [P, LAST], i32), sb("maxi", [P, LAST], i32)

        idx, sidx = sb("idx", [P, RING, G], i32), sb("sidx", [P, RING, G], i32)
        rows = sb("rows", [P, RING, H2, 2 * D])
        srow = sb("srow", [P, RING, EB], i32)
        xT = sb("xT", [D + 1, 2, 2 * EB])
        sums = sb("sums", [P, 2, G, D])
        same = sb("same", [P, 2, G, EB])
        dwin = sb("dwin", [D, RING, EB + 1], i32)
        pen = sb("pen", [D, 2, EB])
        run = sb("run", [D, 2, EB])
        junk = sb("junk", [P, EB])
        xbuf = same[:, :, :, :].rearrange("p a g e -> p (a g e)").rearrange("p (r c d) -> p r c d", r=RING, c=CH)
        store = sb("store", [P, ET * D])
        used = [0]

        def carve(parts, *shape):
            size = 1
            for s in shape:
                size *= s
            lo = used[0]
            used[0] += size
            assert used[0] <= ET * D
            names = "abcd"[:len(shape)]
            spec = f"p ({' '.join(names)}) -> p {' '.join(names)}"
            return store[0:parts, lo:lo + size].rearrange(spec, **dict(zip(names, shape)))

        dh = carve(P, RING, G, D)
        vals = carve(P, 2, G, D)
        tmp = carve(P, 4, H2 * D)
        stats, mv, rstd = carve(P, 2, H2, 6), carve(P, 2, H2, 2), carve(P, 4, H2)
        fh, fa, fo = (carve(P, RING, CH * D) for _ in range(3))
        fv, fw = carve(P, 2, CH * D), carve(P, 2, CH * D)
        fscale = carve(P, 2, 3, CH)

        def wide(name):
            return ctx.enter_context(nc.psum_tensor(name, [P, 1024], fp32))

        pT, pM = wide("pT"), wide("pM")
        pS = [ps("pS0"), ps("pS1")]
        pB = [pM[:, 0:EB], pM[:, EB:2 * EB]]

        loaded, prep, consts_made, sums_made, zero_made = (sem(n) for n in ("loaded", "prep", "consts_made", "sums_made", "zero_made"))
        tables_zeroed, wcat_made, alpha_exp, alpha_made = (sem(n) for n in ("tables_zeroed", "wcat_made", "alpha_exp", "alpha_made"))
        set_up, holds = sem("set_up"), sem("holds")
        p1_gath, p1_dwin, m_srow = sem_ring("p1_gath"), sem_ring("p1_dwin"), sem_ring("m_srow")
        xm_in, xm_out = sem_ring("xm_in"), sem_ring("xm_out")
        p1_xT, p1_xTs, p1_b, p1_run, p1_back, p1_store, p1_idx, p1_chain = (
            sem(n) for n in ("p1_xT", "p1_xTs", "p1_b", "p1_run", "p1_back", "p1_store", "p1_idx", "p1_chain"))
        index_chain, m_ring, m_idx, m_tick, m_seen, m_chain = (sem(n) for n in ("index_chain", "m_ring", "m_idx", "m_tick", "m_seen", "m_chain"))
        m_sc = sem_ring("m_sc", 2)
        phase = {}
        for ph in "ab":
            s = {n: sem_ring(f"{ph}_{n}") for n in ("gath", "srow", "din", "dout")}
            s.update({n: sem(f"{ph}_{n}") for n in (
                "xT", "xTs", "mm", "used", "var", "sd", "same", "vals", "sum", "sums", "idx", "sidx", "sc", "landed", "dh", "chain")})
            phase[ph] = s
        f_in, f_out = sem_ring("f_in"), sem_ring("f_out")
        f_diff, f_used, f_var, f_sd, f_scale, f_done, f_chain, sums_in = (
            sem(n) for n in ("f_diff", "f_used", "f_var", "f_sd", "f_scale", "f_done", "f_chain", "sums_in"))
        block = ctx.enter_context(nc.Block())

        @block.sync
        def _(sp):
            for dram, tile in ((src_col, srci[:, :]), (dst_col, dsti[:, :]), (next_col, nexti[:, :]), (w_col, wcol[:, :]),
                               (w_edge[0:D, :], w1[:, :]), (w_edge[D:2 * D, :], w2[:, :]), (w_res, wcat[0:D, D:2 * D]),
                               (b_edge, wcat[D:D + 1, 0:D]), (b_res, wcat[D:D + 1, D:2 * D]),
                               (alpha.to_broadcast([P, 1]), alph[:, 0:1])):
                sp.dma_start(tile, dram).then_inc(loaded, 16)

            def windows(b, r, k):
                after(sp, p1_run, done(b - RING))
                sp.dma_start(dwin[:, r, :], dst_row[:, ds(b * EB, EB + 1)].to_broadcast([D, EB + 1])).then_inc(p1_dwin[r], 16)
                after(sp, xm_out[r], 16 * k)
                sp.dma_start(xbuf[:, r, :, 0:D], x_rows[:, ds(b * CH, CH), :]).then_inc(xm_in[r], 16)
            over(sp, NB, windows)

            for n, ph in enumerate("ab"):
                s = phase[ph]
                if ph == "a":
                    def src_window(b, r, k):
                        after(sp, m_seen, done(b - RING))
                        sp.dma_start(srow[:, r, :], src_row[:, ds(b * EB, EB)].to_broadcast([P, EB])).then_inc(m_srow[r], 16)
                    over(sp, NB, src_window)
                    for q in range(2):
                        sp.wait_ge(m_sc[q], 64 * NB // 2)
                    sp.wait_ge(m_seen, NB)

                def store_h(b, r, k):
                    sp.wait_ge(s["dh"], done(b))
                    sp.dma_start(h_rows[:, ds((b + n * NB) * G, G), :], dh[:, r, :, :]).then_inc(s["dout"][r], 16)

                def feed(b, r, k):
                    after(sp, s["same"], done(b - RING))
                    sp.dma_start(srow[:, r, :], src_row[:, ds(b * EB, EB)].to_broadcast([P, EB])).then_inc(s["srow"][r], 16)
                    after(sp, s["used"], done(b - RING))
                    sp.dma_start(rows[:, r, G:H2, :], xm_rows[:, ds((b + n * NB) * G, G), :]).then_inc(s["din"][r], 16)
                    if not (isinstance(b, int) and b < RING):
                        store_h(b - RING, r, k)
                over(sp, NB, feed)
                for b in range(NB - RING, NB):
                    store_h(b, b % RING, b // RING)
                for r in range(RING):
                    sp.wait_ge(s["dout"][r], 16 * ((NB - r + RING - 1) // RING))

            sp.wait_ge(sums_in, 1)

            def store_out(b, r, k):
                sp.wait_ge(f_done, done(b))
                sp.dma_start(out_rows[:, ds(b * CH, CH), :], fo[:, r, :].rearrange("p (c d) -> p c d", c=CH)).then_inc(f_out[r], 16)

            def load(b, r, k):
                after(sp, f_used, done(b - RING))
                sp.dma_start(fh[:, r, :].rearrange("p (c d) -> p c d", c=CH), h_rows[:, ds(b * CH, CH), :]).then_inc(f_in[r], 16)
                sp.dma_start(fa[:, r, :].rearrange("p (c d) -> p c d", c=CH), ax2_rows[:, ds(b * CH, CH), :]).then_inc(f_in[r], 16)
                if not (isinstance(b, int) and b < RING):
                    store_out(b - RING, r, k)
            over(sp, NB, load)
            for b in range(NB - RING, NB):
                store_out(b, b % RING, b // RING)
            for r in range(RING):
                sp.wait_ge(f_out[r], 16 * ((NB - r + RING - 1) // RING))

        @block.gpsimd
        def _(pool):
            def hold(sem, value):
                pool.wait_ge(sem, value)
                pool.sem_inc(holds, 1)

            nc.gpsimd.memset(ident[:, :], 0.0).then_inc(prep, 1)
            nc.gpsimd.memset(earlier[:, :, :], 1.0).then_inc(prep, 1)
            pool.wait_ge(prep, 2)
            nc.gpsimd.affine_select(out=ident[:, :], in_=ident[:, :], compare_op=ALU.not_equal, fill=1.0, base=0,
                                    pattern=[[-1, P]], channel_multiplier=1).then_inc(consts_made, 1)
            nc.gpsimd.affine_select(out=earlier[:, :, :], in_=earlier[:, :, :], compare_op=ALU.is_gt, fill=0.0, base=0,
                                    pattern=[[P, G], [-1, EB]], channel_multiplier=1).then_inc(consts_made, 1)
            nc.gpsimd.iota(addi[:, :].rearrange("p (b g) -> p b g", g=G), pattern=[[0, NB + 2], [P, G]], base=NPAD,
                           channel_multiplier=1).then_inc(consts_made, 1)

            def gather_x(b, r, k):
                hold(p1_idx, done(b))
                for g in range(G):
                    nc.gpsimd.indirect_dma_start(rows[:, r, g, 0:D], None, x, at(idx[:, r, g:g + 1])).then_inc(p1_gath[r], 16)
            over(pool, NB, gather_x)

            for r in range(RING):
                pool.wait_ge(xm_out[r], 16 * ((NB - r + RING - 1) // RING))

            def put_max(b, r, k):
                hold(m_ring, done(b))
                hold(m_idx, done(b))
                for g in range(G):
                    nc.gpsimd.indirect_dma_start(xm_halves, at(sidx[:, r, g:g + 1]), sums[:, r % 2, g, :], None,
                                                 bounds_check=2 * NPAD - 1, oob_is_err=False).then_inc(m_sc[r % 2], 16)
                if not (isinstance(b, int) and b == 0):
                    hold(m_sc[1 - r % 2], 64 * pair(r - 1, k))
                    pool.sem_inc(m_tick, 1)
            over(pool, NB, put_max)
            for q in range(2):
                pool.wait_ge(m_sc[q], 64 * NB // 2)
            pool.sem_inc(m_tick, 1)
            pool.wait_ge(tables_zeroed, 16 * 2 * (NB + 1))

            for ph, source, width, target in (("a", xm, 2 * D, ax), ("b", ax, D, ax2)):
                s = phase[ph]

                def gather(r, b):
                    hold(s["idx"], done(b))
                    for g in range(G):
                        nc.gpsimd.indirect_dma_start(rows[:, r, g, 0:width], None, source,
                                                     at(idx[:, r, g:g + 1])).then_inc(s["gath"][r], 16)

                for b in range(RING - 1):
                    gather(b, b)

                def turn(b, r, k):
                    if not (isinstance(b, int) and b + RING - 1 >= NB):
                        gather((r + RING - 1) % RING, b + RING - 1)
                    if not (isinstance(b, int) and b == 0):
                        pool.wait_ge(s["sc"], 64 * b)
                        pool.sem_inc(s["landed"], 1)
                    hold(s["sums"], done(b))
                    hold(s["sidx"], done(b))
                    for g in range(G):
                        nc.gpsimd.indirect_dma_start(target, at(sidx[:, r, g:g + 1]), sums[:, r % 2, g, :], None,
                                                     compute_op=ALU.add).then_inc(s["sc"], 16)
                over(pool, NB, turn)
                pool.wait_ge(s["sc"], 64 * NB)
                pool.sem_inc(s["landed"], 1)
            pool.sem_inc(sums_in, 1)

            def difference(b, r, k):
                pool.wait_ge(f_in[r], 32 * (k + 1))
                after(pool, f_used, done(b - 2))
                nc.gpsimd.tensor_tensor(fv[:, r % 2, :], fa[:, r, :], fh[:, r, :], ALU.subtract).then_inc(f_diff, 1)
            over(pool, NB, difference)

        @block.scalar
        def _(act):
            act.wait_ge(loaded, 160)
            nc.scalar.activation(alph[:, 1:2], alph[:, 0:1], ACT.Exp, scale=-1.0).then_inc(alpha_exp, 1)
            act.wait_ge(zero_made, 1)
            act.wait_ge(set_up, 1)

            def back(b, r, k):
                act.wait_ge(p1_back, done(b))
                nc.scalar.activation(store[:, ds(b * (G * D), G * D)], pS[r % 2][:, 0:G * D], ACT.Copy).then_inc(p1_store, 1)

            def evac(b, r, k):
                q = r % 2
                act.wait_ge(xm_in[r], 16 * (k + 1))
                act.dma_start(xm_rows[:, ds(b * CH, CH), :], xbuf[:, r, :, :]).then_inc(xm_out[r], 16)
                act.wait_ge(p1_xT, done(b))
                after(act, p1_b, done(b - 2))
                nc.scalar.activation(xT[0:D, q, 0:EB], pT[0:D, 0:EB], ACT.Copy).then_inc(p1_xTs, 1)
                if not (isinstance(b, int) and b == 0):
                    back(b - 1, (r - 1) % RING, k)
            over(act, NB, evac)
            back(NB - 1, (NB - 1) % RING, 0)
            act.wait_ge(p1_store, NB)

            def stage(b, r, k):
                after(act, m_tick, done(b - 2))
                nc.scalar.activation(sums[:, r % 2, :, :].rearrange("p g d -> p (g d)"), store[:, ds(b * (G * D), G * D)],
                                     ACT.Copy).then_inc(m_ring, 1)
                for t in (ax, ax2):
                    act.dma_start(t[0:NPAD, :].rearrange("(p c) d -> p c d", p=P)[:, ds(b * CH, CH), :],
                                  zero[:, :].rearrange("p (c d) -> p c d", c=CH)).then_inc(tables_zeroed, 16)
            over(act, NB, stage)
            for t in (ax, ax2):
                act.dma_start(t[NPAD:NT, :].rearrange("(p c) d -> p c d", p=P),
                              zero[:, 0:G * D].rearrange("p (c d) -> p c d", c=G)).then_inc(tables_zeroed, 16)

            for ph, lo in (("a", 0), ("b", G)):
                s = phase[ph]

                def sums_out(b, r, k):
                    act.wait_ge(s["sum"], done(b))
                    after(act, s["landed"], done(b - 2))
                    nc.scalar.activation(sums[:, r % 2, :, :].rearrange("p g d -> p (g d)"), pS[r % 2][:, 0:G * D],
                                         ACT.Copy).then_inc(s["sums"], 1)

                def evac_xT(b, r, k):
                    act.wait_ge(s["xT"], done(b))
                    after(act, s["mm"], done(b - 2))
                    nc.scalar.activation(xT[0:D, r % 2, lo * P:2 * EB], pT[0:D, lo * P:2 * EB], ACT.Copy).then_inc(s["xTs"], 1)

                def step(b, r, k):
                    if not (isinstance(b, int) and b + 1 >= NB):
                        evac_xT(b + 1, (r + 1) % RING, k)
                    if not (isinstance(b, int) and b == 0):
                        sums_out(b - 1, (r - 1) % RING, k)
                    act.wait_ge(s["var"], done(b))
                    nc.scalar.activation(rstd[:, 0, lo:H2], mv[:, r % 2, lo:H2, 1], ACT.Sqrt, bias=eps[:, 0:1]).then_inc(s["sd"], 1)
                if ph == "a":
                    act.wait_ge(m_tick, NB)
                evac_xT(0, 0, 0)
                over(act, NB, step)
                sums_out(NB - 1, (NB - 1) % RING, 0)

            def result(b, r, k):
                act.wait_ge(f_scale, done(b))
                after(act, f_out[r], 16 * k)
                for c in range(CH):
                    ins = nc.scalar.activation(fo[:, r, c * D:(c + 1) * D], fw[:, r % 2, c * D:(c + 1) * D], ACT.Identity,
                                               scale=fscale[:, r % 2, 1, c:c + 1], bias=fscale[:, r % 2, 2, c:c + 1])
                ins.then_inc(f_done, 1)

            def last(b, r, k):
                act.wait_ge(f_var, done(b))
                nc.scalar.activation(fscale[:, r % 2, 0, :], mv[:, r % 2, :, 1], ACT.Sqrt, bias=eps[:, 0:1]).then_inc(f_sd, 1)
                if not (isinstance(b, int) and b == 0):
                    result(b - 1, (r - 1) % RING, k if r else k - 1)
            over(act, NB, last, peel=2)
            result(NB - 1, (NB - 1) % RING, (NB - 1) // RING)

        @block.vector
        def _(dve):
            v = nc.vector
            nc.vector.memset(zero[:, :], 0.0).then_inc(zero_made, 1)
            v.memset(eps[:, :], EPS)
            v.memset(xT[D:D + 1, :, :], 1.0)
            v.memset(xbuf[:, :, :, D:2 * D], -BIG).then_inc(set_up, 1)
            dve.wait_ge(loaded, 160)
            v.tensor_tensor(wcat[0:D, 0:D], w1[:, :], w2[:, :], ALU.subtract).then_inc(wcat_made, 1)
            dve.wait_ge(alpha_exp, 1)
            ch = Chain(dve, alpha_made)
            ch.begin(0, 3)
            ch.link(v.tensor_scalar_add(alph[:, 2:3], alph[:, 1:2], 1.0))
            ch.link(v.reciprocal(alph[:, 3:4], alph[:, 2:3]))
            ch.link(v.tensor_scalar(alph[:, 2:3], alph[:, 3:4], 1e-7, 1.0 - 1e-7, ALU.max, ALU.min))
            ch.end()
            dve.wait_ge(consts_made, 3)
            ch = Chain(dve, index_chain)
            ch.begin(0, 5)
            ch.link(v.tensor_copy(srcf[:, :], srci[:, :]))
            ch.link(v.tensor_tensor(seen[:, :], nexti[:, :], dsti[:, :], ALU.not_equal))
            ch.link(v.tensor_scalar(maxi[:, :], dsti[:, :], 2.0, float(1 - SKIP), ALU.mult, ALU.add))
            ch.link(v.tensor_tensor(maxi[:, :], maxi[:, :], seen[:, :], ALU.mult))
            ch.link(v.tensor_scalar(maxi[:, :], maxi[:, :], 1.0, float(SKIP), ALU.mult, ALU.add))
            ch.end()

            def columns(ring, source, b, r, sem):
                if isinstance(b, int) and b >= NB:
                    return
                v.tensor_copy(ring[:, r, :], source[:, ds(b * G, G)]).then_inc(sem, 1)

            for b in range(RING):
                columns(idx, srci, b, b, p1_idx)
            ch = Chain(dve, p1_chain)

            def scan(b, r, k):
                q = r % 2
                ch.begin(b, 2)
                dve.wait_ge(p1_dwin[r], 16 * (k + 1))
                ch.link(v.tensor_tensor(pen[:, q, :], dwin[:, r, 0:EB], dwin[:, r, 1:EB + 1], ALU.subtract))
                ch.link(v.tensor_scalar(pen[:, q, :], pen[:, q, :], -1.0, BIG, ALU.max, ALU.mult))
                dve.wait_ge(p1_b, done(b))
                columns(idx, srci, b + RING, r, p1_idx)
                after(dve, p1_back, done(b - 2))
                first = isinstance(b, int) and b == 0
                v.tensor_tensor_scan(run[:, q, :], pen[:, q, :], pB[q][0:D, :],
                                     -BIG if first else run[:, 1 - q, EB - 1:EB], ALU.add, ALU.max).then_inc(p1_run, 1)
                dve.wait_ge(p1_run, done(b))
                ch.end()
            over(dve, NB, scan)

            ch = Chain(dve, m_chain)

            def count(b, r, k):
                ch.begin(b, G)
                after(dve, m_tick, done(b - RING))
                columns(sidx, maxi, b, r, m_idx)
                dve.wait_ge(m_srow[r], 16 * (k + 1))
                for g in range(G):
                    w = (g + 1) * P
                    ch.link(v.scalar_tensor_tensor(out=junk[:, 0:w], in0=srow[:, r, 0:w], scalar=srcf[:, ds(b * G + g, 1)],
                                                   in1=earlier[:, g, 0:w], op0=ALU.is_equal, op1=ALU.mult,
                                                   accum_out=seen[:, ds(b * G + g, 1)]))
                v.sem_inc(m_seen, 1)
                ch.end()
            over(dve, NB, count)

            ch = Chain(dve, index_chain)
            ch.base, ch.size, ch.n = 5, 4, 0
            v.memset(seen[:, ET:LAST], 0.0)
            ch.link(v.tensor_scalar(seen[:, 0:ET], seen[:, 0:ET], 1.0, None, ALU.min))
            ch.link(v.tensor_tensor(srcf[:, :], addi[:, :], srcf[:, :], ALU.subtract))
            ch.link(v.tensor_tensor(srcf[:, :], srcf[:, :], seen[:, :], ALU.mult))
            ch.link(v.tensor_tensor(addi[:, :], srcf[:, :], srci[:, :], ALU.add))
            ch.end()
            v.tensor_copy(srcf[:, :], srci[:, :]).then_inc(sums_made, 1)
            dve.wait_ge(sums_made, 1)

            for q in range(2):
                dve.wait_ge(m_sc[q], 64 * NB // 2)
            v.memset(xT[D:D + 1, :, EB:2 * EB], 1.0).then_inc(set_up, 1)

            for n, (ph, lo) in enumerate((("a", 0), ("b", G))):
                s = phase[ph]
                ch = Chain(dve, s["chain"])
                width = (H2 - lo) * D

                def compare(b, r, k):
                    dve.wait_ge(s["srow"][r], 16 * (k + 1))
                    after(dve, s["sum"], done(b - 2))
                    for g in range(G):
                        ins = v.tensor_scalar(same[:, r % 2, g, :], srow[:, r, :], srcf[:, ds(b * G + g, 1)], None, ALU.is_equal)
                    ins.then_inc(s["same"], 1)

                def step(b, r, k):
                    q = r % 2
                    ch.begin(b, 8 if ph == "a" else 7)
                    t = [tmp[:, j, lo * D:H2 * D] for j in range(4)]
                    t3 = [u.rearrange("p (g d) -> p g d", d=D) for u in t]
                    product = pM[:, :].rearrange("p (g d) -> p g d", d=2 * D)[:, lo:H2, :]
                    if ph == "b":
                        dve.wait_ge(s["gath"][r], 64 * (k + 1))
                        after(dve, s["sum"], done(b - 2))
                        v.tensor_tensor(vals[:, q, :, :], rows[:, r, 0:G, 0:D],
                                        wcol[:, ds(b * G, G)].rearrange("p (g o) -> p g o", o=1).to_broadcast([P, G, D]),
                                        ALU.mult).then_inc(s["vals"], 1)
                    dve.wait_ge(s["mm"], done(b))
                    v.tensor_tensor(t3[1], product[:, :, D:2 * D], rows[:, r, lo:H2, 0:D], ALU.add)
                    ch.link(v.tensor_tensor(t3[0], product[:, :, 0:D], rows[:, r, lo:H2, D:2 * D], ALU.add))
                    v.sem_inc(s["used"], 1)
                    columns(idx, dsti, b + RING, r, s["idx"])
                    ch.link(v.tensor_scalar(t[2], t[0], FMAX, None, ALU.is_le))
                    ch.link(v.scalar_tensor_tensor(out=t[3], in0=t[0], scalar=FMAX, in1=t[2], op0=ALU.min, op1=ALU.mult))
                    ch.link(v.scalar_tensor_tensor(out=t[0], in0=t[3], scalar=0.0, in1=t[1], op0=ALU.max, op1=ALU.add))
                    for g in range(lo, H2):
                        ins = v.bn_stats(stats[:, q, g, :], tmp[:, 0, g * D:(g + 1) * D])
                    ch.link(ins)
                    v.sem_inc(holds, 1)
                    for g in range(lo, H2):
                        ins = v.bn_aggr(mv[:, q, g, :], stats[:, q, g, :])
                    ins.then_inc(s["var"], 1)
                    after(dve, s["landed"], done(b - RING))
                    columns(sidx, addi, b, r, s["sidx"])
                    if not (isinstance(b, int) and b + 1 >= NB):
                        compare(b + 1, (r + 1) % RING, k + (r + 1) // RING)
                    dve.wait_ge(s["sd"], done(b))
                    ch.link(v.reciprocal(rstd[:, 1, lo:H2], rstd[:, 0, lo:H2]))
                    if ph == "a":
                        ch.link(v.tensor_tensor(rstd[:, 2, 0:G], rstd[:, 1, 0:G], wcol[:, ds(b * G, G)], ALU.mult))
                        for g in range(G):
                            ins = v.tensor_scalar(vals[:, q, g, :], tmp[:, 0, g * D:(g + 1) * D], mv[:, q, g, 0:1], rstd[:, 2, g:g + 1],
                                                  ALU.subtract, ALU.mult)
                        ins.then_inc(s["vals"], 1)
                    after(dve, s["dout"][r], 16 * k)
                    for g in range(G, H2):
                        ins = v.tensor_scalar(dh[:, r, g - G, :], tmp[:, 0, g * D:(g + 1) * D], mv[:, q, g, 0:1], rstd[:, 1, g:g + 1],
                                              ALU.subtract, ALU.mult)
                    ch.link(ins)
                    v.sem_inc(s["dh"], 1)
                    ch.end()

                if ph == "b":
                    dve.wait_ge(phase["a"]["landed"], NB)
                    v.tensor_scalar(wcol[:, :], wcol[:, :], alph[:, 2:3], None, ALU.mult).then_inc(alpha_made, 1)
                    dve.wait_ge(alpha_made, 4)
                for b in range(RING):
                    columns(idx, dsti, b, b, s["idx"])
                compare(0, 0, 0)
                over(dve, NB, step)

            ch = Chain(dve, f_chain)

            def scale(b, r, k):
                q = r % 2
                dve.wait_ge(f_sd, done(b))
                ch.link(v.reciprocal(fscale[:, q, 1, :], fscale[:, q, 0, :]))
                v.scalar_tensor_tensor(out=fscale[:, q, 2, :], in0=mv[:, q, :, 0], scalar=-1.0, in1=fscale[:, q, 1, :],
                                       op0=ALU.mult, op1=ALU.mult).then_inc(f_scale, 1)

            def last(b, r, k):
                q = r % 2
                first = isinstance(b, int) and b == 0
                ch.begin(b, 5)
                dve.wait_ge(f_diff, done(b))
                d, t = fv[:, q, :], tmp
                ch.link(v.tensor_scalar(t[:, 0, :], d, 0.0, 10.0, ALU.max, ALU.min))
                ch.link(v.scalar_tensor_tensor(out=t[:, 1, :], in0=d, scalar=0.0, in1=t[:, 0, :], op0=ALU.min, op1=ALU.add))
                after(dve, f_done, done(b - 2))
                ch.link(v.scalar_tensor_tensor(out=fw[:, q, :], in0=t[:, 1, :], scalar=-10.0, in1=fh[:, r, :], op0=ALU.max, op1=ALU.add))
                v.sem_inc(f_used, 1)
                for c in range(CH):
                    ins = v.bn_stats(stats[:, q, c, :], fw[:, q, c * D:(c + 1) * D])
                ch.link(ins)
                v.sem_inc(holds, 1)
                for c in range(CH):
                    ins = v.bn_aggr(mv[:, q, c, :], stats[:, q, c, :])
                ins.then_inc(f_var, 1)
                if first:
                    ch.n += 1
                    v.sem_inc(f_chain, 1)
                else:
                    scale(b - 1, (r - 1) % RING, k)
                ch.end()
            over(dve, NB, last)
            ch.begin(NB, 5)
            scale(NB - 1, (NB - 1) % RING, 0)

        @block.tensor
        def _(pe):
            pe.wait_ge(consts_made, 3)
            pe.wait_ge(loaded, 160)
            pe.wait_ge(set_up, 1)
            pe.wait_ge(wcat_made, 1)

            def hold(sem, value):
                if not (isinstance(value, int) and value <= 0):
                    pe.wait_ge(sem, value)
                    pe.sem_inc(holds, 1)

            def turn_back(b, r, k):
                q = r % 2
                hold(p1_run, done(b))
                hold(p1_store, done(b - 2))
                for g in range(G):
                    ins = nc.tensor.transpose(pS[q][:, g * D:(g + 1) * D], run[:, q, g * P:(g + 1) * P], ident[0:D, 0:D])
                ins.then_inc(p1_back, 1)

            def first(b, r, k):
                q = r % 2
                hold(p1_gath[r], 64 * (k + 1))
                hold(p1_xTs, done(b - 1))
                for g in range(G):
                    ins = nc.tensor.transpose(pT[0:D, g * P:(g + 1) * P], rows[:, r, g, 0:D], ident[:, :])
                ins.then_inc(p1_xT, 1)
                hold(p1_xTs, done(b))
                hold(p1_run, done(b - 2))
                nc.tensor.matmul(pB[q][0:D, :], w2[:, :], xT[0:D, q, 0:EB], start=True, stop=True).then_inc(p1_b, 1)
                if not (isinstance(b, int) and b == 0):
                    turn_back(b - 1, (r - 1) % RING, k)
            over(pe, NB, first)
            turn_back(NB - 1, (NB - 1) % RING, 0)
            pe.wait_ge(set_up, 2)

            for ph, lo in (("a", 0), ("b", G)):
                s = phase[ph]

                def add_up(b, r, k):
                    q = r % 2
                    hold(s["vals"], done(b))
                    hold(s["same"], done(b))
                    hold(s["sums"], done(b - 2))
                    for i in range(G):
                        for j in range(G):
                            ins = nc.tensor.matmul(pS[q][:, i * D:(i + 1) * D], same[:, q, j, i * P:(i + 1) * P],
                                                   vals[:, q, j, :], start=(j == 0), stop=(j == G - 1))
                    ins.then_inc(s["sum"], 1)

                def turn(b, r, k):
                    if ph == "a":
                        hold(s["gath"][r], 64 * (k + 1))
                    hold(s["din"][r], 16 * (k + 1))
                    hold(s["xTs"], done(b - 1))
                    for g in range(lo, H2):
                        ins = nc.tensor.transpose(pT[0:D, g * P:(g + 1) * P], rows[:, r, g, 0:D], ident[:, :])
                    ins.then_inc(s["xT"], 1)

                def step(b, r, k):
                    q = r % 2
                    hold(s["xTs"], done(b))
                    hold(s["used"], done(b - 1))
                    for g in range(lo, H2):
                        ins = nc.tensor.matmul(pM[:, g * 2 * D:(g + 1) * 2 * D], xT[:, q, g * P:(g + 1) * P], wcat[:, :],
                                               start=True, stop=True)
                    ins.then_inc(s["mm"], 1)
                    if not (isinstance(b, int) and b + 1 >= NB):
                        turn(b + 1, (r + 1) % RING, k + (r + 1) // RING)
                    if not (isinstance(b, int) and b == 0):
                        add_up(b - 1, (r - 1) % RING, k)
                turn(0, 0, 0)
                over(pe, NB, step)
                add_up(NB - 1, (NB - 1) % RING, 0)


def kernel(x, src, dst, edge_weight, L0_gnn_W_edge, L0_gnn_b_edge, L0_gnn_W_res, L0_gnn_b_res, L1_gnn_alpha_train):
    import numpy as np
    import concourse.bacc as bacc
    from concourse.bass_utils import run_bass_kernel_spmd

    def padded(a, length, fill):
        full = np.full((length,), fill, a.dtype)
        full[:a.shape[0]] = a
        return full

    def columns(a):
        return np.ascontiguousarray(a.reshape(LAST, P).T)

    x, src, dst, w = (np.asarray(a) for a in (x, src, dst, edge_weight))
    long = LAST * P
    x_full = np.zeros((NPAD, D), x.dtype)
    x_full[:N] = x
    src_p, dst_p, w_p = padded(src, long, 0), padded(dst, long + 1, N), padded(w, long, 0)
    next_p = dst_p[1:].copy()
    next_p[ET * P - 1:] = N + 1
    before = np.full((1, ET * P + 1), -1, dst.dtype)
    before[0, 1:] = dst_p[:ET * P]
    arrays = {
        "x": x_full, "src_col": columns(src_p), "dst_col": columns(dst_p[:long]), "next_col": columns(next_p), "w_col": columns(w_p),
        "src_row": src_p[:ET * P].reshape(1, -1), "dst_row": before,
        "w_edge": np.asarray(L0_gnn_W_edge), "b_edge": np.asarray(L0_gnn_b_edge).reshape(1, D),
        "w_res": np.asarray(L0_gnn_W_res), "b_res": np.asarray(L0_gnn_b_res).reshape(1, D),
        "alpha": np.asarray(L1_gnn_alpha_train).reshape(1, 1),
    }
    arrays = {f"in_{n}": np.ascontiguousarray(a) for n, a in arrays.items()}
    nc = bacc.Bacc("TRN2", target_bir_lowering=False, num_devices=1)
    args = [nc.dram_tensor(n, a.shape, mybir.dt.from_np(a.dtype), kind="ExternalInput").ap() for n, a in arrays.items()]
    out = nc.dram_tensor("out", (NPAD, D), mybir.dt.float32, kind="ExternalOutput").ap()
    program(nc, *args, out)
    got = run_bass_kernel_spmd(nc, [arrays], core_ids=[0]).results[0]["out"]
    return got[:N]
```

```python
import concourse.bass as bass
from concourse import mybir
from contextlib import ExitStack

P = 128
D = 64
N = 100000
E = 50000
G = 4
EB = G * P
NB = -(-E // EB)
ET = NB * G
CH = -(-N // (P * NB))
C = NB * CH
NPAD = P * C
H2 = 2 * G
NT = NPAD + EB
RING = 4
AHEAD = 2
LAST = ET + 2 * G
SKIP = 1 << 23
BIG = 3.0e38
FMAX = 3.4028234663852886e38
EPS = 1e-5


def done(b):
    return b + 1


def pair(r, k):
    return 2 * k + r // 2 + 1


def after(eng, sem, value):
    if not (isinstance(value, int) and value <= 0):
        eng.wait_ge(sem, value)


def over(eng, steps, step, peel=1, tail=0):
    rounds = steps // RING - tail
    for b in range(peel * RING):
        step(b, b % RING, b // RING)
    with eng.Fori(peel, rounds) as k:
        for r in range(RING):
            step(k * RING + r, r, k)
    for b in range(rounds * RING, steps):
        step(b, b % RING, b // RING)


class Chain:

    def __init__(self, eng, sem):
        self.eng, self.sem = eng, sem

    def begin(self, b, size):
        self.base, self.size, self.n = b * size, size, 0

    def mark(self, ins):
        self.n += 1
        ins.then_inc(self.sem, 1)

    def ready(self):
        self.eng.wait_ge(self.sem, self.base + self.n)

    def link(self, ins):
        self.mark(ins)
        self.ready()

    def end(self):
        assert self.n == self.size, self.n


assert 2 * G * NB == C, "the two halves of the edge phases take G nodes of a partition with each batch"


def program(nc, x, src_col, dst_col, next_col, w_col, src_row, dst_row, w_edge, b_edge, w_res, b_res, alpha, out):
    fp32, i32, bf16 = mybir.dt.float32, mybir.dt.int32, mybir.dt.bfloat16
    ALU, ACT, AX = mybir.AluOpType, mybir.ActivationFunctionType, mybir.AxisListType
    ds = bass.ds

    def at(ap):
        return bass.IndirectOffsetOnAxis(ap=ap, axis=0)

    ctx = ExitStack()
    with ctx:
        def sb(name, shape, dt=fp32):
            return ctx.enter_context(nc.sbuf_tensor(name, shape, dt))

        def sem(name):
            return ctx.enter_context(nc.semaphore(name))

        def sem_ring(name, n=RING):
            return [sem(f"{name}{i}") for i in range(n)]

        def table(name, rows, cols):
            return nc.dram_tensor(name, [rows, cols], fp32, kind="Internal").ap()

        xm, ax, ax2, hd = table("xm", NPAD, 2 * D), table("ax", NT, D), table("ax2", NT, D), table("hd", NPAD, D)
        xm_halves = xm.rearrange("n (k d) -> (n k) d", k=2)

        def by_partition(t, c):
            return t.rearrange("(p c) d -> p c d", p=P) if c is None else t[0:c, :].rearrange("(p c) d -> p c d", p=P)

        x_rows, xm_rows, h_rows, out_rows = (by_partition(t, None) for t in (x, xm, hd, out))
        ax2_rows = by_partition(ax2, NPAD)

        ident = sb("ident", [P, P])
        earlier = sb("earlier", [P, G, EB], bf16)
        w1, w2 = sb("w1", [D, D]), sb("w2", [D, D])
        wcat = sb("wcat", [D + 1, 2 * D])
        zero = sb("zero", [P, CH * D])
        alph = sb("alph", [P, 4])
        eps, root = sb("eps", [P, 1]), sb("root", [P, 1])
        srci, dsti, nexti = sb("srci", [P, LAST], i32), sb("dsti", [P, LAST], i32), sb("nexti", [P, LAST], i32)
        srcf, wcol, seen = sb("srcf", [P, LAST]), sb("wcol", [P, LAST]), sb("seen", [P, LAST])
        addi, maxi = sb("addi", [P, LAST], i32), sb("maxi", [P, LAST], i32)

        idx, sidx = sb("idx", [P, RING, G], i32), sb("sidx", [P, RING, G], i32)
        rows = sb("rows", [P, RING, H2, 2 * D])
        srow = sb("srow", [P, RING, EB], i32)
        xT = sb("xT", [D + 1, 2, 2 * EB])
        sums = sb("sums", [P, 2, G, D])
        same = sb("same", [P, RING, G, EB], bf16)
        dwin = sb("dwin", [D, RING, EB + 1], i32)
        pen = sb("pen", [D, 2, EB])
        run = sb("run", [D, 2, EB])
        junk = sb("junk", [P, EB])
        xbuf = same[:, :, :, :].rearrange("p r g e -> p (r g e)").bitcast(fp32).rearrange("p (r c d) -> p r c d", r=RING, c=CH)
        parts = sb("parts", [P, 2, G, 3, D], bf16)
        store = sb("store", [P, ET * D])
        used = [0]

        def carve(parts, *shape):
            size = 1
            for s in shape:
                size *= s
            lo = used[0]
            used[0] += size
            assert used[0] <= ET * D
            names = "abcd"[:len(shape)]
            spec = f"p ({' '.join(names)}) -> p {' '.join(names)}"
            return store[0:parts, lo:lo + size].rearrange(spec, **dict(zip(names, shape)))

        made = carve(P, RING, H2, D)
        tmp = carve(P, 3, H2 * D)
        cent, sq = carve(P, 2, H2 * D), carve(P, 2, H2 * D)
        total, factor = carve(P, 2, H2), carve(P, 2, 3, H2)
        rest = carve(P, 3, G * D)
        fh, fa, fo = (carve(P, RING, CH * D) for _ in range(3))
        fv, fpos, fneg = (carve(P, 2, CH * D) for _ in range(3))
        fstat, fmv, fscale = carve(P, 2, CH, 6), carve(P, RING, CH, 2), carve(P, RING, 3, CH)

        def wide(name):
            return ctx.enter_context(nc.psum_tensor(name, [P, 1024], fp32))

        pT, pM = wide("pT"), wide("pM")
        pS = [wide("pS0"), wide("pS1")]
        pR = [t[:, 0:CH * D] for t in (pT, pM, *pS)]
        pB = [pM[:, 0:EB], pM[:, EB:2 * EB]]

        loaded, prep, consts_made, sums_made, zero_made = (sem(n) for n in ("loaded", "prep", "consts_made", "sums_made", "zero_made"))
        tables_zeroed, wcat_made, alpha_exp, alpha_made = (sem(n) for n in ("tables_zeroed", "wcat_made", "alpha_exp", "alpha_made"))
        src_loaded, set_up, holds = sem("src_loaded"), sem("set_up"), sem("holds")
        p1_gath, p1_dwin, m_srow = sem_ring("p1_gath"), sem_ring("p1_dwin"), sem_ring("m_srow")
        xm_in, xm_out = sem_ring("xm_in"), sem_ring("xm_out")
        p1_xT, p1_xTs, p1_b, p1_run, p1_back, p1_store, p1_idx, p1_chain = (
            sem(n) for n in ("p1_xT", "p1_xTs", "p1_b", "p1_run", "p1_back", "p1_store", "p1_idx", "p1_chain"))
        index_chain, m_ring, m_idx, m_tick, m_seen, m_chain = (sem(n) for n in ("index_chain", "m_ring", "m_idx", "m_tick", "m_seen", "m_chain"))
        m_sc = sem_ring("m_sc", 2)
        phase = {}
        for ph in "ab":
            s = {n: sem_ring(f"{ph}_{n}") for n in ("gath", "srow", "din", "dout")}
            s.update({n: sem(f"{ph}_{n}") for n in (
                "xT", "xTs", "mm", "used", "cent", "sq", "var", "sd", "same", "vals", "sum", "sums", "idx", "sidx", "sc", "landed", "dh", "chain")})
            phase[ph] = s
        f_in, f_out = sem_ring("f_in"), sem_ring("f_out")
        f_diff, f_sum, f_stats, f_var, f_sd, f_recip, f_scale, f_done, f_clip, f_first, sums_in = (
            sem(n) for n in ("f_diff", "f_sum", "f_stats", "f_var", "f_sd", "f_recip", "f_scale", "f_done", "f_clip", "f_first", "sums_in"))
        block = ctx.enter_context(nc.Block())

        @block.sync
        def _(sp):
            sp.dma_start(srci[:, :], src_col).then_inc(src_loaded, 16)
            for dram, tile in ((dst_col, dsti[:, :]), (next_col, nexti[:, :]), (w_col, wcol[:, :]),
                               (w_edge[0:D, :], w1[:, :]), (w_edge[D:2 * D, :], w2[:, :]), (w_res, wcat[0:D, D:2 * D]),
                               (b_edge, wcat[D:D + 1, 0:D]), (b_res, wcat[D:D + 1, D:2 * D]),
                               (alpha.to_broadcast([P, 1]), alph[:, 0:1])):
                sp.dma_start(tile, dram).then_inc(loaded, 16)

            def load_x(b, r, k):
                after(sp, xm_out[r], 16 * k)
                sp.dma_start(xbuf[:, r, :, 0:D], x_rows[:, ds(b * CH, CH), :]).then_inc(xm_in[r], 16)

            def windows(b, r, k):
                after(sp, p1_run, done(b - RING))
                sp.dma_start(dwin[:, r, :], dst_row[:, ds(b * EB, EB + 1)].to_broadcast([D, EB + 1])).then_inc(p1_dwin[r], 16)
                if not (isinstance(b, int) and b + AHEAD >= NB):
                    load_x(b + AHEAD, (r + AHEAD) % RING, k + (r + AHEAD) // RING)
            for b in range(AHEAD):
                load_x(b, b, 0)
            over(sp, NB, windows)

            for n, ph in enumerate("ab"):
                s = phase[ph]
                if ph == "a":
                    def src_window(b, r, k):
                        after(sp, m_seen, done(b - RING))
                        sp.dma_start(srow[:, r, :], src_row[:, ds(b * EB, EB)].to_broadcast([P, EB])).then_inc(m_srow[r], 16)
                    over(sp, NB, src_window)
                    for q in range(2):
                        sp.wait_ge(m_sc[q], 64 * NB // 2)
                    sp.wait_ge(m_seen, NB)

                def store_h(b, r, k):
                    sp.wait_ge(s["dh"], done(b))
                    sp.dma_start(h_rows[:, ds((b + n * NB) * G, G), :], made[:, r, G:H2, :]).then_inc(s["dout"][r], 16)

                def feed(b, r, k):
                    after(sp, s["same"], done(b - RING))
                    sp.dma_start(srow[:, r, :], src_row[:, ds(b * EB, EB)].to_broadcast([P, EB])).then_inc(s["srow"][r], 16)
                    after(sp, s["used"], done(b - RING))
                    sp.dma_start(rows[:, r, G:H2, :], xm_rows[:, ds((b + n * NB) * G, G), :]).then_inc(s["din"][r], 16)
                    if not (isinstance(b, int) and b < RING):
                        store_h(b - RING, r, k)
                over(sp, NB, feed)
                for b in range(NB - RING, NB):
                    store_h(b, b % RING, b // RING)
                for r in range(RING):
                    sp.wait_ge(s["dout"][r], 16 * ((NB - r + RING - 1) // RING))

            def load_h(b, r):
                sp.dma_start(fh[:, r, :].rearrange("p (c d) -> p c d", c=CH), h_rows[:, ds(b * CH, CH), :]).then_inc(f_in[r], 16)

            def load(b, r, k):
                if isinstance(b, int) and b == 0:
                    for first in range(RING):
                        load_h(first, first)
                    sp.wait_ge(sums_in, 1)
                elif not (isinstance(b, int) and b < RING):
                    sp.wait_ge(f_diff, done(b - RING))
                    sp.wait_ge(f_first, done(b - RING))
                    load_h(b, r)
                sp.dma_start(fa[:, r, :].rearrange("p (c d) -> p c d", c=CH), ax2_rows[:, ds(b * CH, CH), :]).then_inc(f_in[r], 16)
            over(sp, NB, load)

        @block.gpsimd
        def _(pool):
            def hold(sem, value):
                pool.wait_ge(sem, value)
                pool.sem_inc(holds, 1)

            nc.gpsimd.memset(ident[:, :], 0.0).then_inc(prep, 1)
            nc.gpsimd.memset(earlier[:, :, :], 1.0).then_inc(prep, 1)
            pool.wait_ge(prep, 2)
            nc.gpsimd.affine_select(out=ident[:, :], in_=ident[:, :], compare_op=ALU.not_equal, fill=1.0, base=0,
                                    pattern=[[-1, P]], channel_multiplier=1).then_inc(consts_made, 1)
            nc.gpsimd.affine_select(out=earlier[:, :, :], in_=earlier[:, :, :], compare_op=ALU.is_gt, fill=0.0, base=0,
                                    pattern=[[P, G], [-1, EB]], channel_multiplier=1).then_inc(consts_made, 1)
            nc.gpsimd.iota(addi[:, :].rearrange("p (b g) -> p b g", g=G), pattern=[[0, NB + 2], [P, G]], base=NPAD,
                           channel_multiplier=1).then_inc(consts_made, 1)

            def gather_x(b, r, k):
                hold(p1_idx, done(b))
                for g in range(G):
                    nc.gpsimd.indirect_dma_start(rows[:, r, g, 0:D], None, x, at(idx[:, r, g:g + 1])).then_inc(p1_gath[r], 16)
            over(pool, NB, gather_x)

            for r in range(RING):
                pool.wait_ge(xm_out[r], 16 * ((NB - r + RING - 1) // RING))

            def put_max(b, r, k):
                hold(m_ring, done(b))
                hold(m_idx, done(b))
                for g in range(G):
                    nc.gpsimd.indirect_dma_start(xm_halves, at(sidx[:, r, g:g + 1]), sums[:, r % 2, g, :], None,
                                                 bounds_check=2 * NPAD - 1, oob_is_err=False).then_inc(m_sc[r % 2], 16)
                if not (isinstance(b, int) and b == 0):
                    hold(m_sc[1 - r % 2], 64 * pair(r - 1, k))
                    pool.sem_inc(m_tick, 1)
            over(pool, NB, put_max)
            for q in range(2):
                pool.wait_ge(m_sc[q], 64 * NB // 2)
            pool.sem_inc(m_tick, 1)
            pool.wait_ge(tables_zeroed, 16 * 2 * (NB + 1))

            for ph, source, width, target in (("a", xm, 2 * D, ax), ("b", ax, D, ax2)):
                s = phase[ph]

                def gather(r, b):
                    hold(s["idx"], done(b))
                    for g in range(G):
                        nc.gpsimd.indirect_dma_start(rows[:, r, g, 0:width], None, source,
                                                     at(idx[:, r, g:g + 1])).then_inc(s["gath"][r], 16)

                for b in range(RING - 1):
                    gather(b, b)

                def turn(b, r, k):
                    if not (isinstance(b, int) and b + RING - 1 >= NB):
                        gather((r + RING - 1) % RING, b + RING - 1)
                    if not (isinstance(b, int) and b == 0):
                        pool.wait_ge(s["sc"], 64 * b)
                        pool.sem_inc(s["landed"], 1)
                    hold(s["sums"], done(b))
                    hold(s["sidx"], done(b))
                    for g in range(G):
                        nc.gpsimd.indirect_dma_start(target, at(sidx[:, r, g:g + 1]), sums[:, r % 2, g, :], None,
                                                     compute_op=ALU.add).then_inc(s["sc"], 16)
                over(pool, NB, turn, tail=1)
                pool.wait_ge(s["sc"], 64 * NB)
                pool.sem_inc(s["landed"], 1)
            pool.sem_inc(sums_in, 1)

            def difference(b, r, k):
                pool.wait_ge(f_in[r], 32 * (k + 1))
                after(pool, f_clip, done(b - 2))
                nc.gpsimd.tensor_tensor(fv[:, r % 2, :], fa[:, r, :], fh[:, r, :], ALU.subtract).then_inc(f_diff, 1)
            over(pool, NB, difference)

        @block.scalar
        def _(act):
            act.wait_ge(loaded, 144)
            nc.scalar.activation(alph[:, 1:2], alph[:, 0:1], ACT.Exp, scale=-1.0).then_inc(alpha_exp, 1)
            act.wait_ge(zero_made, 1)
            act.wait_ge(set_up, 1)
            nc.scalar.activation(root[:, :], eps[:, :], ACT.Sqrt)

            def back(b, r, k):
                act.wait_ge(p1_back, done(b))
                nc.scalar.activation(store[:, ds(b * (G * D), G * D)], pS[r % 2][:, 0:G * D], ACT.Copy).then_inc(p1_store, 1)

            def store_x(b, r, k):
                act.wait_ge(xm_in[r], 16 * (k + 1))
                act.dma_start(xm_rows[:, ds(b * CH, CH), :], xbuf[:, r, :, :]).then_inc(xm_out[r], 16)

            def fill(b, r):
                nc.scalar.activation(sums[:, r % 2, :, :].rearrange("p g d -> p (g d)"), store[:, ds(b * (G * D), G * D)],
                                     ACT.Copy).then_inc(m_ring, 1)

            def evac(b, r, k):
                q = r % 2
                if isinstance(b, int) and b == NB - 2:
                    for first in range(2):
                        fill(first, first)
                act.wait_ge(p1_xT, done(b))
                after(act, p1_b, done(b - 2))
                nc.scalar.activation(xT[0:D, q, 0:EB], pT[0:D, 0:EB], ACT.Copy).then_inc(p1_xTs, 1)
                if not (isinstance(b, int) and b + AHEAD >= NB):
                    store_x(b + AHEAD, (r + AHEAD) % RING, k + (r + AHEAD) // RING)
                if not (isinstance(b, int) and b == 0):
                    back(b - 1, (r - 1) % RING, k)
            def zeros(b):
                for t in (ax, ax2):
                    act.dma_start(t[0:NPAD, :].rearrange("(p c) d -> p c d", p=P)[:, ds(b * CH, CH), :],
                                  zero[:, :].rearrange("p (c d) -> p c d", c=CH)).then_inc(tables_zeroed, 16)

            for b in range(AHEAD):
                store_x(b, b, 0)
            for b in range(2):
                zeros(b)
            over(act, NB, evac)
            back(NB - 1, (NB - 1) % RING, 0)
            act.wait_ge(p1_store, NB)

            def stage(b, r, k):
                if not (isinstance(b, int) and b < 2):
                    act.wait_ge(m_tick, done(b - 2))
                    fill(b, r)
                    zeros(b)
            over(act, NB, stage)
            for t in (ax, ax2):
                act.dma_start(t[NPAD:NT, :].rearrange("(p c) d -> p c d", p=P),
                              zero[:, 0:G * D].rearrange("p (c d) -> p c d", c=G)).then_inc(tables_zeroed, 16)

            for ph, lo in (("a", 0), ("b", G)):
                s = phase[ph]

                def sums_out(b, r, k):
                    act.wait_ge(s["sum"], done(b))
                    after(act, s["landed"], done(b - 2))
                    nc.scalar.activation(sums[:, r % 2, :, :], pS[r % 2][:, :].rearrange("p (g c) -> p g c", g=G)[:, :, 0:D],
                                         ACT.Copy).then_inc(s["sums"], 1)

                def evac_xT(b, r, k):
                    act.wait_ge(s["xT"], done(b))
                    after(act, s["mm"], done(b - 2))
                    nc.scalar.activation(xT[0:D, r % 2, lo * P:2 * EB], pT[0:D, lo * P:2 * EB], ACT.Copy).then_inc(s["xTs"], 1)

                def step(b, r, k):
                    if not (isinstance(b, int) and b + 1 >= NB):
                        evac_xT(b + 1, (r + 1) % RING, k)
                    if not (isinstance(b, int) and b == 0):
                        sums_out(b - 1, (r - 1) % RING, k)
                    q = r % 2
                    act.wait_ge(s["cent"], done(b))
                    nc.scalar.activation(sq[:, q, lo * D:H2 * D], cent[:, q, lo * D:H2 * D], ACT.Square).then_inc(s["sq"], 1)
                    act.wait_ge(s["var"], done(b))
                    nc.scalar.activation(factor[:, q, 0, lo:H2], total[:, 1, lo:H2], ACT.Sqrt, scale=1.0 / D,
                                         bias=eps[:, 0:1]).then_inc(s["sd"], 1)
                if ph == "a":
                    act.wait_ge(m_tick, NB)
                evac_xT(0, 0, 0)
                over(act, NB, step)
                sums_out(NB - 1, (NB - 1) % RING, 0)

            def result(b, r, k):
                act.wait_ge(f_scale, done(b))
                after(act, f_out[r], 16 * k)
                for c in range(CH):
                    ins = nc.scalar.activation(fo[:, r, c * D:(c + 1) * D], pR[r][:, c * D:(c + 1) * D], ACT.Identity,
                                               scale=fscale[:, r, 1, c:c + 1], bias=fscale[:, r, 2, c:c + 1])
                ins.then_inc(f_done, 1)

            def store_out(b, r):
                act.wait_ge(f_done, done(b))
                act.dma_start(out_rows[:, ds(b * CH, CH), :], fo[:, r, :].rearrange("p (c d) -> p c d", c=CH)).then_inc(f_out[r], 16)

            def last(b, r, k):
                peeled = b if isinstance(b, int) else NB
                act.wait_ge(f_var, done(b))
                nc.scalar.activation(fscale[:, r, 0, :], fmv[:, r, :, 1], ACT.Sqrt, bias=eps[:, 0:1]).then_inc(f_sd, 1)
                if peeled >= 1:
                    result(b - 1, (r - 1) % RING, k if r else k - 1)
                if peeled >= 2:
                    store_out(b - 2, (r - 2) % RING)
            over(act, NB, last, peel=2)
            result(NB - 1, (NB - 1) % RING, (NB - 1) // RING)
            for b in (NB - 2, NB - 1):
                store_out(b, b % RING)
            for r in range(RING):
                act.wait_ge(f_out[r], 16 * ((NB - r + RING - 1) // RING))

        @block.vector
        def _(dve):
            v = nc.vector

            def columns(ring, source, b, r, sem):
                if isinstance(b, int) and b >= NB:
                    return
                v.tensor_copy(ring[:, r, :], source[:, ds(b * G, G)]).then_inc(sem, 1)

            dve.wait_ge(src_loaded, 16)
            for b in range(RING):
                columns(idx, srci, b, b, p1_idx)
            nc.vector.memset(zero[:, :], 0.0).then_inc(zero_made, 1)
            v.memset(eps[:, :], EPS)
            v.memset(xT[D:D + 1, :, :], 1.0)
            v.memset(xbuf[:, :, :, D:2 * D], -BIG).then_inc(set_up, 1)
            dve.wait_ge(loaded, 144)
            v.tensor_tensor(wcat[0:D, 0:D], w1[:, :], w2[:, :], ALU.subtract).then_inc(wcat_made, 1)
            dve.wait_ge(consts_made, 3)
            v.tensor_tensor(wcat[0:D, D:2 * D], wcat[0:D, D:2 * D], ident[0:D, 0:D], ALU.add).then_inc(wcat_made, 1)
            dve.wait_ge(alpha_exp, 1)
            ch = Chain(dve, alpha_made)
            ch.begin(0, 3)
            ch.link(v.tensor_scalar_add(alph[:, 2:3], alph[:, 1:2], 1.0))
            ch.link(v.reciprocal(alph[:, 3:4], alph[:, 2:3]))
            ch.link(v.tensor_scalar(alph[:, 2:3], alph[:, 3:4], 1e-7, 1.0 - 1e-7, ALU.max, ALU.min))
            ch.end()
            dve.wait_ge(consts_made, 3)
            ch = Chain(dve, index_chain)
            ch.begin(0, 5)
            ch.link(v.tensor_copy(srcf[:, :], srci[:, :]))
            ch.link(v.tensor_tensor(seen[:, :], nexti[:, :], dsti[:, :], ALU.not_equal))
            ch.link(v.tensor_scalar(maxi[:, :], dsti[:, :], 2.0, float(1 - SKIP), ALU.mult, ALU.add))
            ch.link(v.tensor_tensor(maxi[:, :], maxi[:, :], seen[:, :], ALU.mult))
            ch.link(v.tensor_scalar(maxi[:, :], maxi[:, :], 1.0, float(SKIP), ALU.mult, ALU.add))
            ch.end()

            for b in range(RING):
                columns(sidx, maxi, b, b, m_idx)
            ch = Chain(dve, p1_chain)

            def scan(b, r, k):
                q = r % 2
                ch.begin(b, 2)
                dve.wait_ge(p1_dwin[r], 16 * (k + 1))
                ch.link(v.tensor_tensor(pen[:, q, :], dwin[:, r, 0:EB], dwin[:, r, 1:EB + 1], ALU.subtract))
                ch.link(v.tensor_scalar(pen[:, q, :], pen[:, q, :], -1.0, BIG, ALU.max, ALU.mult))
                dve.wait_ge(p1_b, done(b))
                columns(idx, srci, b + RING, r, p1_idx)
                after(dve, p1_back, done(b - 2))
                first = isinstance(b, int) and b == 0
                v.tensor_tensor_scan(run[:, q, :], pen[:, q, :], pB[q][0:D, :],
                                     -BIG if first else run[:, 1 - q, EB - 1:EB], ALU.add, ALU.max).then_inc(p1_run, 1)
                dve.wait_ge(p1_run, done(b))
                ch.end()
            over(dve, NB, scan)

            for b in range(RING):
                columns(idx, dsti, b, b, phase["a"]["idx"])

            ch = Chain(dve, m_chain)

            def count(b, r, k):
                ch.begin(b, G)
                if not (isinstance(b, int) and b < RING):
                    dve.wait_ge(m_tick, done(b - RING))
                    columns(sidx, maxi, b, r, m_idx)
                dve.wait_ge(m_srow[r], 16 * (k + 1))
                for g in range(G):
                    w = (g + 1) * P
                    ch.link(v.scalar_tensor_tensor(out=junk[:, 0:w], in0=srow[:, r, 0:w], scalar=srcf[:, ds(b * G + g, 1)],
                                                   in1=earlier[:, g, 0:w], op0=ALU.is_equal, op1=ALU.mult,
                                                   accum_out=seen[:, ds(b * G + g, 1)]))
                v.sem_inc(m_seen, 1)
                ch.end()
            over(dve, NB, count)

            ch = Chain(dve, index_chain)
            ch.base, ch.size, ch.n = 5, 4, 0
            v.memset(seen[:, ET:LAST], 0.0)
            ch.link(v.tensor_scalar(seen[:, 0:ET], seen[:, 0:ET], 1.0, None, ALU.min))
            ch.link(v.tensor_tensor(srcf[:, :], addi[:, :], srcf[:, :], ALU.subtract))
            ch.link(v.tensor_tensor(srcf[:, :], srcf[:, :], seen[:, :], ALU.mult))
            ch.link(v.tensor_tensor(addi[:, :], srcf[:, :], srci[:, :], ALU.add))
            ch.end()
            v.tensor_copy(srcf[:, :], srci[:, :]).then_inc(sums_made, 1)
            dve.wait_ge(sums_made, 1)

            for n, (ph, lo) in enumerate((("a", 0), ("b", G))):
                s = phase[ph]
                ch = Chain(dve, s["chain"])

                def compare(b, r, k, g):
                    w = (g + 1) * P
                    if g == 0:
                        dve.wait_ge(s["srow"][r], 16 * (k + 1))
                        after(dve, s["sum"], done(b - RING))
                    ins = v.tensor_scalar(same[:, r, g, 0:w], srow[:, r, 0:w], srcf[:, ds(b * G + g, 1)], None, ALU.is_equal)
                    if g == G - 1:
                        ins.then_inc(s["same"], 1)

                def step(b, r, k):
                    q = r % 2
                    ch.begin(b, 10)

                    def of_groups(ap):
                        return ap.rearrange("p (g o) -> p g o", o=1).to_broadcast([P, ap.shape[1], D])

                    def next_compare(g):
                        if not (isinstance(b, int) and b + 1 >= NB):
                            compare(b + 1, (r + 1) % RING, k + (r + 1) // RING, g)
                    t = [tmp[:, j, lo * D:H2 * D] for j in range(3)]
                    t3 = [u.rearrange("p (g d) -> p g d", d=D) for u in t]
                    c, c3 = cent[:, q, lo * D:H2 * D], cent[:, q, lo * D:H2 * D].rearrange("p (g d) -> p g d", d=D)
                    product = pM[:, :].rearrange("p (g d) -> p g d", d=2 * D)[:, lo:H2, :]
                    value = made[:, r, 0:G, :]
                    after(dve, s["dout"][r], 16 * k)
                    if ph == "b":
                        dve.wait_ge(s["gath"][r], 64 * (k + 1))
                        ch.mark(v.tensor_tensor(value, rows[:, r, 0:G, 0:D], of_groups(wcol[:, ds(b * G, G)]), ALU.mult))

                    def split(stage):
                        if stage == 0:
                            after(dve, s["sum"], done(b - 2))
                        hi, mid, low = (parts[:, q, :, i, :] for i in range(3))
                        flat = [rest[:, i, :].rearrange("p (g d) -> p g d", g=G) for i in range(2)]
                        ch.ready()
                        if stage == 0:
                            ch.mark(v.tensor_copy(hi, value))
                        elif stage == 1:
                            ch.mark(v.tensor_tensor(flat[0], value, hi, ALU.subtract))
                        elif stage == 2:
                            ch.mark(v.tensor_copy(mid, flat[0]))
                        else:
                            v.tensor_tensor(low, flat[0], mid, ALU.subtract).then_inc(s["vals"], 1)

                    dve.wait_ge(s["mm"], done(b))
                    if ph == "b":
                        split(0)
                    ins = v.tensor_tensor(t3[0], product[:, :, 0:D], rows[:, r, lo:H2, D:2 * D], ALU.add)
                    if ph == "b":
                        split(1)
                    ch.mark(ins)
                    after(dve, s["landed"], done(b - RING))
                    columns(sidx, addi, b, r, s["sidx"])
                    ch.ready()
                    ch.mark(v.scalar_tensor_tensor(out=t[1], in0=t[0], scalar=FMAX, in1=t[0], op0=ALU.is_le, op1=ALU.mult))
                    if ph == "b":
                        split(2)
                    else:
                        next_compare(0)
                        ch.ready()
                    ins = v.scalar_tensor_tensor(out=t3[2], in0=t3[1], scalar=0.0, in1=product[:, :, D:2 * D], op0=ALU.max, op1=ALU.add)
                    ch.mark(ins)
                    if ph == "b":
                        split(3)
                        next_compare(0)
                    next_compare(1)
                    ch.ready()
                    v.sem_inc(s["used"], 1)
                    columns(idx, dsti, b + RING, r, s["idx"])
                    ch.link(v.tensor_reduce(total[:, 0, lo:H2], t3[2], AX.X, ALU.add))
                    v.scalar_tensor_tensor(out=c3, in0=of_groups(total[:, 0, lo:H2]), scalar=-1.0 / D, in1=t3[2],
                                           op0=ALU.mult, op1=ALU.add).then_inc(s["cent"], 1)
                    next_compare(2)
                    dve.wait_ge(s["sq"], done(b))
                    v.tensor_reduce(total[:, 1, lo:H2], sq[:, q, lo * D:H2 * D].rearrange("p (g d) -> p g d", d=D), AX.X,
                                    ALU.add).then_inc(s["var"], 1)
                    next_compare(3)
                    dve.wait_ge(s["sd"], done(b))
                    ch.link(v.reciprocal(factor[:, q, 1, lo:H2], factor[:, q, 0, lo:H2]))
                    if ph == "a":
                        ch.link(v.tensor_tensor(factor[:, q, 1, 0:G], factor[:, q, 1, 0:G], wcol[:, ds(b * G, G)], ALU.mult))
                    ch.mark(v.tensor_tensor(made[:, r, lo:H2, :], c3, of_groups(factor[:, q, 1, lo:H2]), ALU.mult))
                    if ph == "a":
                        for stage in range(4):
                            split(stage)
                    else:
                        ch.ready()
                    v.sem_inc(s["dh"], 1)
                    ch.end()

                if ph == "b":
                    v.tensor_scalar(wcol[:, :], wcol[:, :], alph[:, 2:3], None, ALU.mult).then_inc(alpha_made, 1)
                    dve.wait_ge(alpha_made, 4)
                if ph == "b":
                    for b in range(RING):
                        columns(idx, dsti, b, b, s["idx"])
                for g in range(G):
                    compare(0, 0, 0, g)
                if ph == "a":
                    for q in range(2):
                        dve.wait_ge(m_sc[q], 64 * NB // 2)
                else:
                    dve.wait_ge(phase["a"]["landed"], NB)
                over(dve, NB, step, tail=1)


            def statistics(b, r):
                dve.wait_ge(f_sum, done(b))
                v.sem_inc(holds, 1)
                for c in range(CH):
                    ins = v.bn_stats(fstat[:, r % 2, c, :], pR[r][:, c * D:(c + 1) * D])
                ins.then_inc(f_stats, 1)

            def moments(b, r):
                dve.wait_ge(f_stats, done(b))
                v.sem_inc(holds, 1)
                for c in range(CH):
                    ins = v.bn_aggr(fmv[:, r, c, :], fstat[:, r % 2, c, :])
                ins.then_inc(f_var, 1)

            def inverse(b, r):
                dve.wait_ge(f_sd, done(b))
                v.reciprocal(fscale[:, r, 1, :], fscale[:, r, 0, :]).then_inc(f_recip, 1)

            def shift(b, r):
                dve.wait_ge(f_recip, done(b))
                v.scalar_tensor_tensor(out=fscale[:, r, 2, :], in0=fmv[:, r, :, 0], scalar=-1.0, in1=fscale[:, r, 1, :],
                                       op0=ALU.mult, op1=ALU.mult).then_inc(f_scale, 1)

            def last(b, r, k):
                peeled = b if isinstance(b, int) else NB
                q = r % 2
                dve.wait_ge(f_diff, done(b))
                after(dve, f_sum, done(b - 2))
                v.tensor_scalar(fpos[:, q, :], fv[:, q, :], 0.0, 10.0, ALU.max, ALU.min)
                v.tensor_scalar(fneg[:, q, :], fv[:, q, :], 0.0, -10.0, ALU.min, ALU.max).then_inc(f_clip, 1)
                if peeled >= 1:
                    statistics(b - 1, (r - 1) % RING)
                if peeled >= 2:
                    inverse(b - 2, (r - 2) % RING)
                if peeled >= 1:
                    moments(b - 1, (r - 1) % RING)
                if peeled >= 2:
                    shift(b - 2, (r - 2) % RING)
            over(dve, NB, last)
            statistics(NB - 1, (NB - 1) % RING)
            inverse(NB - 2, (NB - 2) % RING)
            moments(NB - 1, (NB - 1) % RING)
            shift(NB - 2, (NB - 2) % RING)
            inverse(NB - 1, (NB - 1) % RING)
            shift(NB - 1, (NB - 1) % RING)

        @block.tensor
        def _(pe):
            pe.wait_ge(consts_made, 3)
            pe.wait_ge(loaded, 144)
            pe.wait_ge(set_up, 1)
            pe.wait_ge(wcat_made, 2)

            def hold(sem, value):
                if not (isinstance(value, int) and value <= 0):
                    pe.wait_ge(sem, value)
                    pe.sem_inc(holds, 1)

            def turn_back(b, r, k):
                q = r % 2
                hold(p1_run, done(b))
                hold(p1_store, done(b - 2))
                for g in range(G):
                    ins = nc.tensor.transpose(pS[q][:, g * D:(g + 1) * D], run[:, q, g * P:(g + 1) * P], ident[0:D, 0:D])
                ins.then_inc(p1_back, 1)

            def first(b, r, k):
                q = r % 2
                hold(p1_gath[r], 64 * (k + 1))
                hold(p1_xTs, done(b - 1))
                for g in range(G):
                    ins = nc.tensor.transpose(pT[0:D, g * P:(g + 1) * P], rows[:, r, g, 0:D], ident[:, :])
                ins.then_inc(p1_xT, 1)
                hold(p1_xTs, done(b))
                hold(p1_run, done(b - 2))
                nc.tensor.matmul(pB[q][0:D, :], w2[:, :], xT[0:D, q, 0:EB], start=True, stop=True).then_inc(p1_b, 1)
                if not (isinstance(b, int) and b == 0):
                    turn_back(b - 1, (r - 1) % RING, k)
            over(pe, NB, first)
            turn_back(NB - 1, (NB - 1) % RING, 0)

            for ph, lo in (("a", 0), ("b", G)):
                s = phase[ph]

                def add_up(b, r, k):
                    q = r % 2
                    hold(s["vals"], done(b))
                    hold(s["same"], done(b))
                    hold(s["sums"], done(b - 2))
                    for i in range(G):
                        for j in range(i, G):
                            for part in range(3):
                                ins = nc.tensor.matmul(pS[q][:, i * 4 * D:i * 4 * D + D], same[:, r, j, i * P:(i + 1) * P],
                                                       parts[:, q, j, part, :], start=(j == i and part == 0),
                                                       stop=(j == G - 1 and part == 2))
                    ins.then_inc(s["sum"], 1)

                def turn(b, r, k):
                    if ph == "a":
                        hold(s["gath"][r], 64 * (k + 1))
                    hold(s["din"][r], 16 * (k + 1))
                    hold(s["xTs"], done(b - 1))
                    for g in range(lo, H2):
                        ins = nc.tensor.transpose(pT[0:D, g * P:(g + 1) * P], rows[:, r, g, 0:D], ident[:, :])
                    ins.then_inc(s["xT"], 1)

                def step(b, r, k):
                    q = r % 2
                    hold(s["xTs"], done(b))
                    hold(s["used"], done(b - 1))
                    for g in range(lo, H2):
                        ins = nc.tensor.matmul(pM[:, g * 2 * D:(g + 1) * 2 * D], xT[:, q, g * P:(g + 1) * P], wcat[:, :],
                                               start=True, stop=True)
                    ins.then_inc(s["mm"], 1)
                    if not (isinstance(b, int) and b + 1 >= NB):
                        turn(b + 1, (r + 1) % RING, k + (r + 1) // RING)
                    if not (isinstance(b, int) and b == 0):
                        add_up(b - 1, (r - 1) % RING, k)
                turn(0, 0, 0)
                over(pe, NB, step)
                add_up(NB - 1, (NB - 1) % RING, 0)

            for ph in "ab":
                pe.wait_ge(phase[ph]["sums"], NB)

            def add_parts(b, r, k):
                hold(f_in[r], 32 * (k + 1))
                hold(f_done, done(b - RING))
                nc.tensor.matmul(pR[r], ident[:, :], fh[:, r, :], start=True, stop=False).then_inc(f_first, 1)
                hold(f_clip, done(b))
                nc.tensor.matmul(pR[r], ident[:, :], fpos[:, r % 2, :], start=False, stop=False)
                nc.tensor.matmul(pR[r], ident[:, :], fneg[:, r % 2, :], start=False, stop=True).then_inc(f_sum, 1)
            over(pe, NB, add_parts)


def kernel(x, src, dst, edge_weight, L0_gnn_W_edge, L0_gnn_b_edge, L0_gnn_W_res, L0_gnn_b_res, L1_gnn_alpha_train):
    import numpy as np
    import concourse.bacc as bacc
    from concourse.bass_utils import run_bass_kernel_spmd

    def padded(a, length, fill):
        full = np.full((length,), fill, a.dtype)
        full[:a.shape[0]] = a
        return full

    def columns(a):
        return np.ascontiguousarray(a.reshape(LAST, P).T)

    x, src, dst, w = (np.asarray(a) for a in (x, src, dst, edge_weight))
    long = LAST * P
    x_full = np.zeros((NPAD, D), x.dtype)
    x_full[:N] = x
    src_p, dst_p, w_p = padded(src, long, 0), padded(dst, long + 1, N), padded(w, long, 0)
    next_p = dst_p[1:].copy()
    next_p[ET * P - 1:] = N + 1
    before = np.full((1, ET * P + 1), -1, dst.dtype)
    before[0, 1:] = dst_p[:ET * P]
    arrays = {
        "x": x_full, "src_col": columns(src_p), "dst_col": columns(dst_p[:long]), "next_col": columns(next_p), "w_col": columns(w_p),
        "src_row": src_p[:ET * P].reshape(1, -1), "dst_row": before,
        "w_edge": np.asarray(L0_gnn_W_edge), "b_edge": np.asarray(L0_gnn_b_edge).reshape(1, D),
        "w_res": np.asarray(L0_gnn_W_res), "b_res": np.asarray(L0_gnn_b_res).reshape(1, D),
        "alpha": np.asarray(L1_gnn_alpha_train).reshape(1, 1),
    }
    arrays = {f"in_{n}": np.ascontiguousarray(a) for n, a in arrays.items()}
    nc = bacc.Bacc("TRN2", target_bir_lowering=False, num_devices=1)
    args = [nc.dram_tensor(n, a.shape, mybir.dt.from_np(a.dtype), kind="ExternalInput").ap() for n, a in arrays.items()]
    out = nc.dram_tensor("out", (NPAD, D), mybir.dt.float32, kind="ExternalOutput").ap()
    program(nc, *args, out)
    got = run_bass_kernel_spmd(nc, [arrays], core_ids=[0]).results[0]["out"]
    return got[:N]
```
